# Optimizing a Trainium2 kernel written in Bass

```python
import numpy as np
import jax
import jax.numpy as jnp

def _softmax(x, axis=-1):
    return jax.nn.softmax(x, axis=axis)

def _gelu(x):
    return jax.nn.gelu(x, approximate=True)

def _silu(x):
    return jax.nn.silu(x)

def _sigmoid(x):
    return jax.nn.sigmoid(x)

def _layernorm(x, axis=-1, eps=1e-05):
    m = jnp.mean(x, axis=axis, keepdims=True)
    v = jnp.var(x, axis=axis, keepdims=True)
    return (x - m) / jnp.sqrt(v + eps)

def _scatter_add(tgt, idx, src, axis=0):
    return tgt.at[idx].add(src)

def _segment_sum(src, seg, n):
    return jax.ops.segment_sum(src, seg, n)
kernel_name = 'mk_adaln_attn_ffn_d1_seqx_r8_d28025'

def setup_inputs(seed: int=0):
    np.random.seed(seed)
    _w = jnp.asarray

    def _rec_inputs():
        import jax
        import jax.numpy as jnp
        _rk = jax.random.key(seed)
        x = -0.0002071 + 1 * jax.random.normal(jax.random.fold_in(_rk, 1), (16, 128, 128), jnp.float32)
        _lenS = 128 - jax.random.randint(jax.random.fold_in(_rk, 7), (16,), 0, max(1, 128 // 4) + 1, jnp.int32)
        _lenS2 = 128 - jax.random.randint(jax.random.fold_in(_rk, 8), (16,), 0, max(1, 128 // 4) + 1, jnp.int32)
        cond_8 = jax.random.uniform(jax.random.fold_in(_rk, 11), (16, 8), jnp.float32, 0.0, 0.983423)
        return (x, cond_8)
    x, cond_8 = _rec_inputs()

    def _L0_cond_setup():
        import jax, jax.numpy as jnp
        import numpy as np
        R = 16
        ALPHA = 32.0
        SCALING = ALPHA / R
        key = jax.random.key(seed)
        ks = jax.random.split(key, 6)
        B, T, C, O, E = (16, 1500, 128, 128, 8)
        x = jax.random.normal(ks[0], (B, T, C), dtype=jnp.float32)
        w = jax.random.uniform(ks[1], (B, E), dtype=jnp.float32)
        W_base = jax.random.normal(ks[2], (O, C), dtype=jnp.float32) * 0.02
        b_base = jax.random.normal(ks[3], (O,), dtype=jnp.float32) * 0.02
        As = jax.random.normal(ks[4], (E, R, C), dtype=jnp.float32) * 0.02
        Bs = jax.random.normal(ks[5], (E, O, R), dtype=jnp.float32) * 0.02
        return {'x': x, 'w': w, 'W_base': W_base, 'b_base': b_base, 'As': As, 'Bs': Bs}
    _L0_cond_all = _L0_cond_setup()
    _L0_cond_in = {k: v for k, v in _L0_cond_all.items() if k in ('W_base', 'b_base', 'As', 'Bs')}
    del _L0_cond_all

    def _L0_attn_setup():
        import jax, jax.numpy as jnp
        import numpy as np
        D_MODEL = 128
        N_HEAD = 16
        HEAD_DIM = D_MODEL // N_HEAD
        LN_EPS = 1e-05

        def _split_heads(y, B, T):
            return y.reshape(B, T, N_HEAD, HEAD_DIM).transpose(1, 0, 2, 3)

        def _layernorm(y, gamma, beta):
            mu = jnp.mean(y, axis=-1, keepdims=True)
            var = jnp.mean(jnp.square(y - mu), axis=-1, keepdims=True)
            return (y - mu) * jax.lax.rsqrt(var + LN_EPS) * gamma + beta
        key = jax.random.key(seed)
        ks = jax.random.split(key, 8)
        B, T = (2, 256)
        s = 1.0 / np.sqrt(D_MODEL)
        x = jax.random.normal(ks[0], (B, T, D_MODEL), dtype=jnp.float32)
        Wq = jax.random.uniform(ks[1], (D_MODEL, D_MODEL), jnp.float32, -s, s)
        Wk = jax.random.uniform(ks[2], (D_MODEL, D_MODEL), jnp.float32, -s, s)
        Wv = jax.random.uniform(ks[3], (D_MODEL, D_MODEL), jnp.float32, -s, s)
        Wg = jax.random.uniform(ks[4], (D_MODEL, D_MODEL), jnp.float32, -s, s)
        Wo = jax.random.uniform(ks[5], (D_MODEL, D_MODEL), jnp.float32, -s, s)
        gamma = jnp.ones((D_MODEL,), jnp.float32)
        beta = jnp.zeros((D_MODEL,), jnp.float32)
        return {'x': x, 'Wq': Wq, 'Wk': Wk, 'Wv': Wv, 'Wg': Wg, 'Wo': Wo, 'gamma': gamma, 'beta': beta}
    _L0_attn_all = _L0_attn_setup()
    _L0_attn_in = {k: v for k, v in _L0_attn_all.items() if k in ('Wq', 'Wk', 'Wv', 'Wg', 'Wo', 'gamma', 'beta')}
    del _L0_attn_all

    def _L0_cond2_setup():
        import jax, jax.numpy as jnp
        import numpy as np
        B, S, D = (16, 256, 128)
        E, H = (8, 256)
        key = jax.random.key(seed)
        ks = jax.random.split(key, 8)
        scale = 0.02
        x = jax.random.normal(ks[0], (B, S, D), dtype=jnp.float32)
        opcode_onehot = jax.random.uniform(ks[1], (B, E), dtype=jnp.float32)
        W_up = jax.random.normal(ks[2], (E, H, D), dtype=jnp.float32) * scale
        b_up = jnp.zeros((E, H), dtype=jnp.float32)
        W_gate = jax.random.normal(ks[3], (E, H, D), dtype=jnp.float32) * scale
        b_gate = jnp.zeros((E, H), dtype=jnp.float32)
        W_down = jax.random.normal(ks[4], (E, D, H), dtype=jnp.float32) * scale
        b_down = jnp.zeros((E, D), dtype=jnp.float32)
        return {'x': x, 'opcode_onehot': opcode_onehot, 'W_up': W_up, 'b_up': b_up, 'W_gate': W_gate, 'b_gate': b_gate, 'W_down': W_down, 'b_down': b_down}
    _L0_cond2_all = _L0_cond2_setup()
    _L0_cond2_in = {k: v for k, v in _L0_cond2_all.items() if k in ('W_up', 'b_up', 'W_gate', 'b_gate', 'W_down', 'b_down')}
    del _L0_cond2_all

    def _L0_ffn_setup():
        import jax, jax.numpy as jnp
        import numpy as np
        TOP_K = 2
        key = jax.random.key(seed)
        ks = jax.random.split(key, 6)
        B, T, H, E, F = (2, 256, 128, 8, 512)
        s = 0.02
        return {'hidden_states': jax.random.normal(ks[0], (B, T, H), dtype=jnp.float32), 'router_w': jax.random.normal(ks[1], (E, H), dtype=jnp.float32) * s, 'w1': jax.random.normal(ks[2], (E, F, H), dtype=jnp.float32) * s, 'b1': jax.random.normal(ks[3], (E, F), dtype=jnp.float32) * s, 'w2': jax.random.normal(ks[4], (E, H, F), dtype=jnp.float32) * s, 'b2': jax.random.normal(ks[5], (E, H), dtype=jnp.float32) * s}
    _L0_ffn_all = _L0_ffn_setup()
    _L0_ffn_in = {k: v for k, v in _L0_ffn_all.items() if k in ('router_w', 'w1', 'b1', 'w2', 'b2')}
    del _L0_ffn_all
    return {'x': x, 'cond_8': cond_8, 'L0_cond_W_base': _L0_cond_in['W_base'], 'L0_cond_b_base': _L0_cond_in['b_base'], 'L0_cond_As': _L0_cond_in['As'], 'L0_cond_Bs': _L0_cond_in['Bs'], 'L0_attn_Wq': _L0_attn_in['Wq'], 'L0_attn_Wk': _L0_attn_in['Wk'], 'L0_attn_Wv': _L0_attn_in['Wv'], 'L0_attn_Wg': _L0_attn_in['Wg'], 'L0_attn_Wo': _L0_attn_in['Wo'], 'L0_attn_gamma': _L0_attn_in['gamma'], 'L0_attn_beta': _L0_attn_in['beta'], 'L0_cond2_W_up': _L0_cond2_in['W_up'], 'L0_cond2_b_up': _L0_cond2_in['b_up'], 'L0_cond2_W_gate': _L0_cond2_in['W_gate'], 'L0_cond2_b_gate': _L0_cond2_in['b_gate'], 'L0_cond2_W_down': _L0_cond2_in['W_down'], 'L0_cond2_b_down': _L0_cond2_in['b_down'], 'L0_ffn_router_w': _L0_ffn_in['router_w'], 'L0_ffn_w1': _L0_ffn_in['w1'], 'L0_ffn_b1': _L0_ffn_in['b1'], 'L0_ffn_w2': _L0_ffn_in['w2'], 'L0_ffn_b2': _L0_ffn_in['b2']}

def reference(x, cond_8, L0_cond_W_base, L0_cond_b_base, L0_cond_As, L0_cond_Bs, L0_attn_Wq, L0_attn_Wk, L0_attn_Wv, L0_attn_Wg, L0_attn_Wo, L0_attn_gamma, L0_attn_beta, L0_cond2_W_up, L0_cond2_b_up, L0_cond2_W_gate, L0_cond2_b_gate, L0_cond2_W_down, L0_cond2_b_down, L0_ffn_router_w, L0_ffn_w1, L0_ffn_b1, L0_ffn_w2, L0_ffn_b2):
    import jax
    import jax.numpy as jnp

    def _L0_cond_ref(x, w, W_base, b_base, As, Bs):
        import jax, jax.numpy as jnp
        import numpy as np
        R = 16
        ALPHA = 32.0
        SCALING = ALPHA / R
        out = jnp.einsum('btc,oc->bto', x, W_base) + b_base
        h = jnp.einsum('btc,erc->bter', x, As)
        lora = jnp.einsum('bter,eor,be->bto', h, Bs, w)
        return out + lora * SCALING

    def _L0_attn_ref(x, Wq, Wk, Wv, Wg, Wo, gamma, beta):
        import jax, jax.numpy as jnp
        import numpy as np
        D_MODEL = 128
        N_HEAD = 16
        HEAD_DIM = D_MODEL // N_HEAD
        LN_EPS = 1e-05

        def _split_heads(y, B, T):
            return y.reshape(B, T, N_HEAD, HEAD_DIM).transpose(1, 0, 2, 3)

        def _layernorm(y, gamma, beta):
            mu = jnp.mean(y, axis=-1, keepdims=True)
            var = jnp.mean(jnp.square(y - mu), axis=-1, keepdims=True)
            return (y - mu) * jax.lax.rsqrt(var + LN_EPS) * gamma + beta
        B, T, D = x.shape
        q = _split_heads(jnp.einsum('btd,ed->bte', x, Wq), B, T)
        k = _split_heads(jnp.einsum('btd,ed->bte', x, Wk), B, T)
        v = _split_heads(jnp.einsum('btd,ed->bte', x, Wv), B, T)
        a = jax.nn.sigmoid(_split_heads(jnp.einsum('btd,ed->bte', x, Wg), B, T))

        def step(h, inp):
            q_t, k_t, v_t, a_t = inp
            h = a_t[..., None] * h + k_t[..., None] * v_t[..., None, :]
            y_t = jnp.einsum('bhd,bhde->bhe', q_t, h)
            return (h, y_t)
        h0 = jnp.zeros((B, N_HEAD, HEAD_DIM, HEAD_DIM), x.dtype)
        _, y = jax.lax.scan(step, h0, (q, k, v, a))
        y = y.transpose(1, 0, 2, 3).reshape(B, T, D)
        y = _layernorm(y, gamma, beta)
        return jnp.einsum('btd,ed->bte', y, Wo)

    def _L0_cond2_ref(x, opcode_onehot, W_up, b_up, W_gate, b_gate, W_down, b_down):
        import jax, jax.numpy as jnp
        import numpy as np
        B, S, D = (16, 256, 128)
        E, H = (8, 256)
        expert = jnp.argmax(opcode_onehot, axis=-1)
        wu, bu = (W_up[expert], b_up[expert])
        wg, bg = (W_gate[expert], b_gate[expert])
        wd, bd = (W_down[expert], b_down[expert])
        up = jnp.einsum('bsd,bhd->bsh', x, wu) + bu[:, None, :]
        gate = jnp.einsum('bsd,bhd->bsh', x, wg) + bg[:, None, :]
        hidden = jax.nn.silu(up) * gate
        out = jnp.einsum('bsh,bdh->bsd', hidden, wd) + bd[:, None, :]
        return out

    def _L0_ffn_ref(hidden_states, router_w, w1, b1, w2, b2):
        import jax, jax.numpy as jnp
        import numpy as np
        TOP_K = 2
        x = hidden_states
        router_logits = jnp.einsum('bth,eh->bte', x, router_w)
        topk_values, topk_indices = jax.lax.top_k(router_logits, TOP_K)
        topk_weights = jax.nn.softmax(topk_values.astype(jnp.float32), axis=-1).astype(x.dtype)
        h1 = jnp.einsum('bth,efh->btef', x, w1) + b1
        h1 = jax.nn.gelu(h1, approximate=False)
        expert_outputs = jnp.einsum('btef,ehf->bteh', h1, w2) + b2
        gather_idx = topk_indices[..., None]
        topk_expert_outputs = jnp.take_along_axis(expert_outputs, gather_idx, axis=2)
        mixed_output = jnp.sum(topk_expert_outputs * topk_weights[..., None], axis=2)
        return mixed_output
    x = x + _L0_attn_ref(_L0_cond_ref(x, cond_8, L0_cond_W_base, L0_cond_b_base, L0_cond_As, L0_cond_Bs), L0_attn_Wq, L0_attn_Wk, L0_attn_Wv, L0_attn_Wg, L0_attn_Wo, L0_attn_gamma, L0_attn_beta)
    x = x + _L0_ffn_ref(_L0_cond2_ref(x, cond_8, L0_cond2_W_up, L0_cond2_b_up, L0_cond2_W_gate, L0_cond2_b_gate, L0_cond2_W_down, L0_cond2_b_down), L0_ffn_router_w, L0_ffn_w1, L0_ffn_b1, L0_ffn_w2, L0_ffn_b2)
    return x

_drawn_inputs = setup_inputs


def setup_inputs(seed=0):
    import zlib

    import numpy as np

    out = dict(_drawn_inputs(seed))
    spreads = {'L0_attn_gamma': (1.0, 0.2),
     'L0_attn_beta': (0.0, 0.1),
     'L0_cond2_b_up': (0.0, 0.8),
     'L0_cond2_b_gate': (0.0, 0.8),
     'L0_cond2_b_down': (0.0, 0.496)}
    factors = {'L0_attn_Wg': 2.823,
     'L0_cond2_W_up': 8.0,
     'L0_cond2_W_gate': 8.0,
     'L0_cond2_W_down': 8.0,
     'L0_ffn_router_w': 4.419,
     'L0_ffn_w1': 8.0,
     'L0_ffn_b1': 43.856,
     'L0_ffn_w2': 8.0,
     'L0_ffn_b2': 109.507}
    for name, (base, spread) in spreads.items():
        noise = np.random.default_rng([zlib.crc32(name.encode()), seed]).standard_normal(out[name].shape)
        drawn = base * np.exp(spread * noise) if base else spread * noise
        out[name] = jnp.asarray(drawn.astype(out[name].dtype))
    for name, factor in factors.items():
        out[name] = (out[name] * factor).astype(out[name].dtype)
    return out
```

```python
from contextlib import ExitStack

import numpy as np

import concourse.bass as bass
from concourse import mybir

F32 = mybir.dt.float32
BF16 = mybir.dt.bfloat16
I32 = mybir.dt.int32
U32 = mybir.dt.uint32
ALU = mybir.AluOpType
ACT = mybir.ActivationFunctionType
AX_X = mybir.AxisListType.X

P = 128
NB = 16
E = 8
NH = 16
GB = 4
NG = NB // GB
GT = GB * P
NT = NB * P
H2 = 256
FF = 512
FC = FF // P
TOPK = 2
LN_EPS = 1e-5
LORA_SCALE = 2.0
ROW = P + 2
REGION = NT + P
DUMMY = E * REGION
JOBS = (NT * TOPK + E * (P - 1)) // P
RING = 3
NOWHERE = 1 << 20
BUG, B1O, BDO, B2O, NBIAS = 0, E * 2 * H2, E * (2 * H2 + FF), E * (2 * H2 + FF + P), E * (2 * H2 + FF + 2 * P)
assert JOBS % RING == 0


def adaln_attn_ffn_kernel(nc, xT, w_first, w_rest, w_upgate, w_down, w_1, w_2, w_router, columns,
                          cond_row, cond_T, biases, identity, select, before, ranks, dest, job_no, out):
    v_rows = nc.dram_tensor("v_rows", [NG, P, GT], F32).ap()
    bias_rows = nc.dram_tensor("bias_rows", [3, NBIAS], BF16).ap()
    routed = nc.dram_tensor("routed", [DUMMY + P, ROW], F32).ap()
    mixed = nc.dram_tensor("mixed", [TOPK * NT, P], F32).ap()

    with ExitStack() as ctx:
        def sb(name, shape, dt=F32):
            return ctx.enter_context(nc.sbuf_tensor(name, shape, dt))

        def sem(name):
            return ctx.enter_context(nc.semaphore(name))

        x_sb = sb("x_sb", [P, NT])
        wf = sb("wf", [P, 2 * P])
        wr = sb("wr", [P, 6 * P])
        wug = sb("wug", [P, E * 2 * H2])
        wd = sb("wd", [P, E * 2 * P])
        w1 = sb("w1", [P, E * FF])
        w2 = sb("w2", [P, E * FC * P])
        wrt = sb("wrt", [P, E])
        cols = sb("cols", [P, 3])
        crow_w = sb("crow_w", [1, NB, E])
        ccol = sb("ccol", [P, NB])
        ccol2 = sb("ccol2", [P, NB])
        b_in = sb("b_in", [P, NBIAS // P])
        b_part = sb("b_part", [P, 3, NBIAS // P], BF16)
        b_rest = sb("b_rest", [P, 2, NBIAS // P])
        brow = sb("brow", [P, NBIAS], BF16)
        ident = sb("ident", [P, P])
        sel = sb("sel", [P, E, 32])
        bef_f = sb("bef_f", [P, P])
        bef = sb("bef", [P, P], BF16)
        ones = sb("ones", [P, P], BF16)
        rk = sb("rk", [P, 2, E])
        dst = sb("dst", [P, NB, TOPK], U32)
        jno = sb("jno", [1, 2, JOBS])
        hs = sb("hs", [P, GT])
        xc = sb("xc", [P, GT])
        v_sb = sb("v_sb", [P, GT])
        k_sb = sb("k_sb", [P, NT])
        state = sb("state", [P, 2, E, GT])
        prod = sb("prod", [P, E, GT])
        y_sb = sb("y_sb", [P, GT])
        bst = sb("bst", [P, GB, 6])
        mv = sb("mv", [P, GB, 2])
        var = sb("var", [P, GB])
        sd = sb("sd", [P, GB])
        rstd = sb("rstd", [P, GB])
        z_sb = sb("z_sb", [P, GT])
        zn = sb("zn", [P, GT])
        x1T = sb("x1T", [P, GT])
        cmax = sb("cmax", [1, NB])
        ceq = sb("ceq", [1, NB, E])
        crk = sb("crk", [1, NB])
        cexp = sb("cexp", [1, NB], I32)
        silu_sb = sb("silu_sb", [P, 2, H2])
        hid = sb("hid", [P, 2, H2])
        hidT = sb("hidT", [P, 2, H2])
        cT = sb("cT", [P, GT])
        rows = sb("rows", [P, GB, TOPK, ROW])
        x1 = sb("x1", [P, NB, P])
        lg = sb("lg", [P, GB, E])
        lg2 = sb("lg2", [P, GB, E])
        m1 = sb("m1", [P, GB])
        m2 = sb("m2", [P, GB])
        eq = sb("eq", [P, GB, E])
        rr = sb("rr", [P, GB])
        oh1 = sb("oh1", [P, GB, E])
        oh2 = sb("oh2", [P, GB, E])
        rank = sb("rank", [P, GB, E])
        pick = sb("pick", [P, TOPK, GB, E])
        wdiff = sb("wdiff", [P, GB])
        wgt = sb("wgt", [P, TOPK, GB])
        M = sb("M", [P, GB, E], BF16)
        Mpre = sb("Mpre", [P, GB + 1, E], BF16)
        slot_f = sb("slot_f", [P, TOPK, GB])
        slot = sb("slot", [P, TOPK, GB], U32)
        cnt = sb("cnt", [1, E])
        ctiles = sb("ctiles", [1, E])
        cmp16 = sb("cmp16", [1, E, NB])
        cends = sb("cends", [1, E])
        ones_e = sb("ones_e", [1, E])
        jge = sb("jge", [1, JOBS, E])
        jex = sb("jex", [1, JOBS])
        jst = sb("jst", [1, JOBS])
        jok = sb("jok", [1, JOBS])
        jtmp = sb("jtmp", [1, JOBS])
        jrow = sb("jrow", [1, JOBS], I32)
        jwex = sb("jwex", [1, JOBS], I32)
        padf = sb("padf", [1, E])
        padr = sb("padr", [1, E], I32)
        pad = sb("pad", [P, ROW])
        late = state[:, :, :, :].rearrange("p g e t -> p (g e t)")
        at = [0]

        def carve(*shape):
            n = int(np.prod(shape))
            a = late[:, at[0]:at[0] + n]
            at[0] += n
            assert at[0] <= 2 * E * GT
            return a.rearrange({2: "p (a b) -> p a b", 3: "p (a b c) -> p a b c"}[len(shape)],
                               **dict(zip("abc", shape)))

        jin = carve(RING, ROW)
        jmeta = carve(JOBS, 2)
        jT = carve(RING, P)
        act_sb = carve(RING, FF)
        actT = carve(RING, FF)
        res = carve(RING, P)
        y0 = carve(2, GB * P)
        y1 = carve(2, GB * P)
        jidx = sb("jidx", [P, RING], U32)

        bank = [ctx.enter_context(nc.psum_tensor(f"bank{i}", [P, GT], F32)) for i in range(8)]
        B_XC, B_HK, B_A, B_Q, B_Y = bank[0:5]
        B_ROW, B_W = bank[5:7], bank[7]
        J_H, J_X, J_T, J_O = bank[0:3], bank[3], bank[4], bank[5]

        names = """s_x s_wf s_wr s_c s_ugd s_w12 s_bias_out s_bias_rows s_pad s_padrow s_vst s_scatter s_out
            ones_ready brow_zero before_ready bias_split expert_ready ccol_ready
            pe_h pe_xc pe_v pe_k pe_g pe_q pe_y pe_yt pe_zt pe_o
            act_hs act_xc act_v act_k act_a act_y act_sd act_zn
            kv_ready a_zeroed scanned prod_ready dve_chain stats_ready var_ready z_ready x1_ready
            pe_ug pe_ht pe_c pe_ct pe_l pe_x1 pe_rank pe_cnt
            silu_done hid_ready hidT_ready c_ready cT_ready x1_copied
            lg_copied wdiff_ready wgt_ready chosen placed slot_ready rows_ready jobs_ready
            pe_jx pe_jh pe_jt pe_jo jT_ready jin_free gelu_done actT_ready added""".split()
        S = {n: sem(n) for n in names}
        s_vload = [sem(f"s_vload{e}") for e in range(E)]
        s_job = [sem(f"s_job{r}") for r in range(RING)]
        s_put_idx = [sem(f"s_put_idx{r}") for r in range(RING)]
        s_put_res = [sem(f"s_put_res{r}") for r in range(RING)]
        s_put = [sem(f"s_put{r}") for r in range(RING)]
        s_y = [sem(f"s_y{r}") for r in range(2)]

        block = ctx.enter_context(nc.Block())

        def grp(g):
            return bass.ds(g * GT, GT)

        @block.sync
        def _(sp):
            sp.dma_start(wf[:, :], w_first).then_inc(S["s_wf"], 16)
            for g in range(NG):
                sp.dma_start(x_sb[:, g * GT:(g + 1) * GT], xT[:, g * GT:(g + 1) * GT]).then_inc(S["s_x"], 16)
                if g == 0:
                    sp.dma_start(wr[:, :], w_rest).then_inc(S["s_wr"], 16)
            def spread_v(g, used):
                sp.wait_ge(S["act_v"], g + 1)
                sp.dma_start(v_rows[bass.ds(g, 1), :, :].rearrange("g p t -> p (g t)"), v_sb[:, :]).then_inc(S["s_vst"], 16)
                sp.wait_ge(S["s_vst"], g * 16 + 16)
                for e in range(E):
                    if used is not None:
                        sp.wait_ge(S["prod_ready"], used * E + e + 1)
                    src = v_rows[bass.ds(g, 1), :, :].rearrange("g (h e) t -> (g h) e t", e=E)[:, e, :]
                    sp.dma_start(state[:, bass.ds(g % 2, 1), e, :].rearrange("p g t -> p (g t)"),
                                 src.unsqueeze(1).broadcast_to([NH, E, GT])).then_inc(s_vload[e], 16)

            spread_v(0, None)
            spread_v(1, None)
            sp.dma_start(wug[:, :], w_upgate).then_inc(S["s_ugd"], 16)
            sp.dma_start(wd[:, :], w_down).then_inc(S["s_ugd"], 16)
            sp.dma_start(w1[:, :], w_1).then_inc(S["s_w12"], 16)
            sp.dma_start(w2[:, :], w_2).then_inc(S["s_w12"], 16)
            with sp.Fori(0, NG - 2) as g:
                spread_v(g + 2, g)
            sp.wait_ge(S["s_pad"], 3)
            sp.dma_start(routed[DUMMY:DUMMY + P, :], pad[:, :]).then_inc(S["s_padrow"], 16)
            sp.wait_ge(S["jobs_ready"], 1)
            with sp.Fori(0, E) as e:
                r = sp.value_load(padr[0:1, bass.ds(e, 1)], min_val=0, max_val=DUMMY - P)
                sp.dma_start(routed[bass.ds(r, P), :], pad[:, :]).then_inc(S["s_padrow"], 16)
            sp.wait_ge(S["s_padrow"], 16 * (E + 1))
            sp.wait_ge(S["s_scatter"], 16 * NB * TOPK)
            def load(j, r, free):
                row = sp.value_load(jrow[0:1, bass.ds(j, 1)], min_val=0, max_val=DUMMY)
                if free is not None:
                    sp.wait_ge(S["jin_free"], free)
                sp.dma_start(jin[:, r, :], routed[bass.ds(row, P), :]).then_inc(s_job[r], 16)

            for r in range(RING):
                load(r, r, None)
            with sp.Fori(0, JOBS // RING - 1) as t:
                for r in range(RING):
                    load(t * RING + RING + r, r, t * RING + r + 1)
            for r in range(RING):
                sp.wait_ge(s_put[r], 16 * (JOBS // RING))
            mx = mixed.rearrange("(k b p) d -> k p b d", k=TOPK, p=P)
            ov = out.rearrange("b p d -> p b d")

            def rows_of(y, g):
                return y[:, g % 2, :].rearrange("p (b d) -> p b d", d=P)

            for g in range(NG):
                if g >= 2:
                    sp.wait_ge(S["added"], g - 1)
                    sp.wait_ge(S["s_out"], 16 * (g - 1))
                sp.dma_start(rows_of(y0, g), mx[0, :, g * GB:(g + 1) * GB, :]).then_inc(s_y[g % 2], 16)
                sp.dma_start(rows_of(y1, g), mx[1, :, g * GB:(g + 1) * GB, :]).then_inc(s_y[g % 2], 16)
                if g >= 1:
                    sp.wait_ge(S["added"], g)
                    sp.dma_start(ov[:, (g - 1) * GB:g * GB, :], rows_of(y0, g - 1)).then_inc(S["s_out"], 16)
            sp.wait_ge(S["added"], NG)
            sp.dma_start(ov[:, (NG - 1) * GB:, :], rows_of(y0, NG - 1)).then_inc(S["s_out"], 16)
            sp.wait_ge(S["s_out"], 16 * NG)

        @block.gpsimd
        def _(pool):
            pool.memset(ones[:, :], 1.0).then_inc(S["ones_ready"], 1)
            pool.memset(pad[:, 0:P], 0.0).then_inc(S["s_pad"], 1)
            pool.memset(pad[:, P:P + 1].bitcast(U32), NOWHERE).then_inc(S["s_pad"], 1)
            pool.memset(pad[:, P + 1:ROW], 0.0).then_inc(S["s_pad"], 1)
            pool.memset(brow[:, :].bitcast(U32), 0).then_inc(S["brow_zero"], 1)
            pool.wait_ge(S["bias_split"], 3)
            pool.dma_start(bias_rows.rearrange("k (p n) -> p k n", p=P), b_part[:, :, :]).then_inc(S["s_bias_out"], 16)

            def key_value(g):
                half = g % 2 if isinstance(g, int) else pool.snap(g % 2)
                pool.wait_ge(S["act_k"], g + 1)
                for e in range(E):
                    pool.wait_ge(s_vload[e], g * 16 + 16)
                    st = state[:, bass.ds(half, 1), e, :].rearrange("p g t -> p (g t)")
                    pool.tensor_tensor(st, st, k_sb[:, grp(g)], ALU.mult).then_inc(S["kv_ready"], 1)

            def scatter(groups):
                pool.wait_ge(S["brow_zero"], 1)
                pool.wait_ge(S["slot_ready"], groups)
                pool.wait_ge(S["rows_ready"], groups)
                for i in range(GB):
                    for k in range(TOPK):
                        pool.indirect_dma_start(
                            out=routed, out_offset=bass.IndirectOffsetOnAxis(ap=slot[:, k, i:i + 1], axis=0),
                            in_=rows[:, i, k, :], in_offset=None,
                            bounds_check=DUMMY - 1, oob_is_err=False).then_inc(S["s_scatter"], 16)

            key_value(0)
            pool.wait_ge(S["s_bias_out"], 16)
            pool.wait_ge(S["brow_zero"], 1)
            pool.dma_start(brow[0:3, :], bias_rows).then_inc(S["s_bias_rows"], 16)
            key_value(1)
            with pool.Fori(1, NG - 1) as n:
                key_value(n + 1)
                scatter(n)
            scatter(NG - 1)
            scatter(NG)
            with pool.Fori(1, JOBS // RING + 1) as n:
                for r in range(RING):
                    pool.wait_ge(S["brow_zero"], 1)
                    pool.wait_ge(s_put_idx[r], n)
                    pool.wait_ge(s_put_res[r], n)
                    pool.indirect_dma_start(
                        out=mixed, out_offset=bass.IndirectOffsetOnAxis(ap=jidx[:, r:r + 1], axis=0),
                        in_=res[:, r, :], in_offset=None,
                        bounds_check=TOPK * NT - 1, oob_is_err=False).then_inc(s_put[r], 16)

        @block.scalar
        def _(act):
            act.dma_start(ccol[:, :], cond_T.unsqueeze(1).broadcast_to([E, NH, NB])).then_inc(S["s_c"], 16)
            act.dma_start(cols[:, :], columns).then_inc(S["s_c"], 16)
            act.dma_start(crow_w[:, :, :].rearrange("p b e -> p (b e)"), cond_row).then_inc(S["s_c"], 16)
            act.dma_start(sel[:, :, :].rearrange("p e c -> p (e c)"), select).then_inc(S["s_c"], 16)
            act.dma_start(ident[:, :], identity).then_inc(S["s_c"], 16)
            act.dma_start(bef_f[:, :], before).then_inc(S["s_c"], 16)
            act.dma_start(rk[:, :, :].rearrange("p a e -> p (a e)"), ranks).then_inc(S["s_c"], 16)
            act.dma_start(wrt[:, :], w_router).then_inc(S["s_c"], 16)
            act.dma_start(b_in[:, :], biases).then_inc(S["s_c"], 16)
            act.dma_start(dst[:, :, :].rearrange("p b k -> p (b k)"), dest).then_inc(S["s_c"], 16)
            act.dma_start(jno[:, :, :].rearrange("p j e -> p (j e)"), job_no).then_inc(S["s_c"], 16)
            act.wait_ge(S["s_c"], 16 * 11)
            act.activation(ccol2[:, :], ccol[:, :], ACT.Copy, scale=LORA_SCALE).then_inc(S["ccol_ready"], 1)
            act.wait_ge(S["ccol_ready"], 1)

            def project(g):
                act.wait_ge(S["pe_h"], g + 1)
                for i in range(GB):
                    last = act.activation(hs[:, i * P:(i + 1) * P], B_HK[:, i * P:(i + 1) * P], ACT.Copy,
                                          scale=ccol2[:, bass.ds(g * GB + i, 1)])
                last.then_inc(S["act_hs"], 1)
                act.wait_ge(S["pe_xc"], g + 1)
                act.wait_ge(S["pe_q"], g)
                act.activation(xc[:, :], B_XC[:, :], ACT.Identity, bias=cols[:, 0:1]).then_inc(S["act_xc"], 1)
                act.wait_ge(S["pe_v"], g + 1)
                act.wait_ge(S["s_vst"], g * 16)
                act.activation(v_sb[:, :], B_XC[:, :], ACT.Copy).then_inc(S["act_v"], 1)
                act.wait_ge(S["pe_k"], g + 1)
                act.activation(k_sb[:, grp(g)], B_HK[:, :], ACT.Copy).then_inc(S["act_k"], 1)

            def gate(g):
                act.wait_ge(S["pe_g"], g + 1)
                act.activation(B_A[:, :], B_A[:, :], ACT.Sigmoid).then_inc(S["act_a"], 1)

            def take_y(g):
                act.wait_ge(S["pe_y"], g + 1)
                act.wait_ge(S["pe_yt"], g)
                act.activation(y_sb[:, :], B_Y[:, :], ACT.Copy).then_inc(S["act_y"], 1)

            def norm(g):
                act.wait_ge(S["var_ready"], g + 1)
                act.activation(sd[:, :], var[:, :], ACT.Sqrt).then_inc(S["act_sd"], 1)
                act.wait_ge(S["pe_zt"], g + 1)
                act.wait_ge(S["pe_o"], g)
                act.activation(zn[:, :], B_Y[:, :], ACT.Identity, bias=cols[:, 2:3], scale=cols[:, 1:2]).then_inc(S["act_zn"], 1)

            def silu(g, n):
                act.wait_ge(S["pe_ug"], g * GB + n + 1)
                act.wait_ge(S["hid_ready"], g * GB + (n - 1 if n else 0))
                act.activation(silu_sb[:, n % 2, :], B_ROW[n % 2][:, 0:H2], ACT.Silu).then_inc(S["silu_done"], 1)

            def take_hidT(g, n):
                act.wait_ge(S["pe_ht"], g * GB + n + 1)
                act.wait_ge(S["pe_c"], g * GB + (n - 1 if n else 0))
                act.activation(hidT[:, n % 2, :], B_ROW[n % 2][:, 0:H2], ACT.Copy).then_inc(S["hidT_ready"], 1)

            def take_c(g, n):
                act.wait_ge(S["pe_c"], g * GB + n + 1)
                if n == 0:
                    act.wait_ge(S["s_scatter"], g * (16 * GB * TOPK))
                act.activation(rows[:, n, 0, 0:P], B_ROW[n % 2][:, 0:P], ACT.Copy).then_inc(S["c_ready"], 1)

            def conditional(g):
                silu(g, 0)
                silu(g, 1)
                for n in range(0, GB, 2):
                    take_hidT(g, n)
                    take_hidT(g, n + 1)
                    take_c(g, n)
                    take_c(g, n + 1)
                    if n + 2 < GB:
                        silu(g, n + 2)
                        silu(g, n + 3)
                act.wait_ge(S["pe_ct"], g + 1)
                act.activation(cT[:, :], B_W[:, :], ACT.Copy).then_inc(S["cT_ready"], 1)
                act.wait_ge(S["pe_x1"], g + 1)
                act.activation(x1[:, bass.ds(g * GB, GB), :].rearrange("p b d -> p (b d)"),
                               B_W[:, :], ACT.Copy).then_inc(S["x1_copied"], 1)
                act.wait_ge(S["wdiff_ready"], g + 1)
                act.activation(wgt[:, 1, :], wdiff[:, :], ACT.Sigmoid)
                act.activation(wgt[:, 0, :], wdiff[:, :], ACT.Sigmoid, scale=-1.0).then_inc(S["wgt_ready"], 1)

            def tail(g, ahead, final):
                take_y(g)
                if not final:
                    gate(g + 1)
                norm(g)
                if ahead:
                    project(g + 2)
                conditional(g)

            project(0)
            gate(0)
            project(1)
            with act.Fori(0, NG - 2) as g:
                tail(g, True, False)
            tail(NG - 2, False, False)
            tail(NG - 1, False, True)

            with act.Fori(0, JOBS // RING) as t:
                for r in range(RING):
                    act.wait_ge(S["pe_jh"], t * RING + r + 1)
                    act.wait_ge(S["pe_jt"], t * RING + (r - 2 if r >= 2 else 0))
                    act.activation(act_sb[:, r, :], J_H[r][:, :], ACT.Gelu).then_inc(S["gelu_done"], 1)

        @block.vector
        def _(dve):
            done = [0]

            def link(ins, base=0):
                done[0] += 1
                ins.then_inc(S["dve_chain"], 1)
                dve.wait_ge(S["dve_chain"], base + done[0])

            dve.wait_ge(S["s_c"], 16 * 11)
            link(dve.reduce_max(cmax[:, :], crow_w[:, :, :], AX_X))
            link(dve.tensor_tensor(ceq[:, :, :], crow_w[:, :, :], cmax[:, :].unsqueeze(2).broadcast_to([1, NB, E]), ALU.is_equal))
            link(dve.tensor_tensor(ceq[:, :, :], ceq[:, :, :], rk[0:1, 0:1, :].broadcast_to([1, NB, E]), ALU.mult))
            link(dve.reduce_max(crk[:, :], ceq[:, :, :], AX_X))
            dve.tensor_scalar(cexp[:, :], crk[:, :], -1.0, float(E), ALU.mult, ALU.add).then_inc(S["expert_ready"], 1)
            dve.tensor_copy(b_part[:, 0, :], b_in[:, :]).then_inc(S["bias_split"], 1)
            dve.wait_ge(S["bias_split"], 1)
            link(dve.tensor_tensor(b_rest[:, 0, :], b_in[:, :], b_part[:, 0, :], ALU.subtract))
            dve.tensor_copy(b_part[:, 1, :], b_rest[:, 0, :]).then_inc(S["bias_split"], 1)
            dve.wait_ge(S["bias_split"], 2)
            link(dve.tensor_tensor(b_rest[:, 1, :], b_rest[:, 0, :], b_part[:, 1, :], ALU.subtract))
            dve.tensor_copy(b_part[:, 2, :], b_rest[:, 1, :]).then_inc(S["bias_split"], 1)
            dve.tensor_copy(bef[:, :], bef_f[:, :]).then_inc(S["before_ready"], 1)
            link(dve.memset(ones_e[:, :], 1.0))
            link(dve.memset(Mpre[:, GB, :], 0.0))
            START = done[0]

            def unit(g, product, e):
                st = state[:, bass.ds(g % 2, 1), e, :].rearrange("p g t -> p (g t)")
                if not product:
                    dve.wait_ge(S["kv_ready"], g * E + e + 1)
                    dve.tensor_tensor_scan(st, B_A[:, :], st, 0.0, ALU.mult, ALU.add).then_inc(S["scanned"], 1)
                else:
                    dve.wait_ge(S["scanned"], g * E + e + 1)
                    if e == 0:
                        dve.wait_ge(S["pe_y"], g)
                    dve.tensor_tensor(prod[:, e, :], st, B_Q[:, :], ALU.mult).then_inc(S["prod_ready"], 1)

            def recur(g, between):
                dve.wait_ge(S["act_a"], g + 1)
                dve.memset(B_A[:, :].rearrange("p (b t) -> p b t", t=P)[:, :, 0:1], 0.0).then_inc(S["a_zeroed"], 1)
                dve.wait_ge(S["a_zeroed"], g + 1)
                unit(g, False, 0)
                dve.wait_ge(S["pe_q"], g + 1)
                for e in range(1, E):
                    unit(g, False, e)
                    unit(g, True, e - 1)
                    between(e)
                unit(g, True, E - 1)

            LINKS = 19

            def norm_stats(g, link):
                dve.wait_ge(S["pe_yt"], g + 1)
                for i in range(GB):
                    last = dve.bn_stats(bst[:, i, :], B_Y[:, i * P:(i + 1) * P])
                last.then_inc(S["stats_ready"], 1)
                n_stats = g + 1 if isinstance(g, int) else dve.snap(g + 1)
                dve.wait_ge(S["s_c"], 16 * 11)
                dve.wait_ge(S["stats_ready"], n_stats)
                for i in range(GB):
                    last = dve.bn_aggr(mv[:, i, :], bst[:, i, :])
                link(last)
                dve.tensor_scalar(var[:, :], mv[:, :, 1], LN_EPS, None, ALU.add).then_inc(S["var_ready"], 1)

            def norm_apply(g, link):
                dve.wait_ge(S["act_sd"], g + 1)
                link(dve.reciprocal(rstd[:, :], sd[:, :]))
                for i in range(GB):
                    last = dve.tensor_scalar(z_sb[:, i * P:(i + 1) * P], B_Y[:, i * P:(i + 1) * P],
                                             mv[:, i, 0:1], rstd[:, i:i + 1], ALU.subtract, ALU.mult)
                last.then_inc(S["z_ready"], 1)

            def residual(g):
                dve.wait_ge(S["pe_o"], g + 1)
                dve.wait_ge(S["pe_x1"], g)
                dve.tensor_tensor(x1T[:, :], x_sb[:, grp(g)], B_Y[:, :], ALU.add).then_inc(S["x1_ready"], 1)

            def hidden(g, n):
                dve.wait_ge(S["silu_done"], g * GB + n + 1)
                dve.wait_ge(S["pe_ht"], g * GB + (n - 1 if n else 0))
                dve.tensor_tensor(hid[:, n % 2, :], silu_sb[:, n % 2, :], B_ROW[n % 2][:, H2:2 * H2],
                                  ALU.mult).then_inc(S["hid_ready"], 1)

            def spread(ap):
                return ap.unsqueeze(2).broadcast_to([P, GB, E])

            def route(g, link):
                dve.wait_ge(S["pe_l"], g + 1)
                dve.tensor_copy(lg[:, :, :].rearrange("p b e -> p (b e)"), B_W[:, 0:GB * E]).then_inc(S["lg_copied"], 1)
                dve.wait_ge(S["lg_copied"], g + 1)
                for scores, most, onehot in ((lg, m1, oh1), (lg2, m2, oh2)):
                    link(dve.reduce_max(most[:, :], scores[:, :, :], AX_X))
                    link(dve.tensor_tensor(eq[:, :, :], scores[:, :, :], spread(most[:, :]), ALU.is_equal))
                    link(dve.tensor_tensor(eq[:, :, :], eq[:, :, :], rk[:, 0:1, :].broadcast_to([P, GB, E]), ALU.mult))
                    link(dve.reduce_max(rr[:, :], eq[:, :, :], AX_X))
                    link(dve.tensor_tensor(onehot[:, :, :], rk[:, 0:1, :].broadcast_to([P, GB, E]), spread(rr[:, :]), ALU.is_equal))
                    if scores is lg:
                        link(dve.scalar_tensor_tensor(lg2[:, :, :].rearrange("p b e -> p (b e)"),
                                                      oh1[:, :, :].rearrange("p b e -> p (b e)"), -3.0e38,
                                                      lg[:, :, :].rearrange("p b e -> p (b e)"), ALU.mult, ALU.add))
                dve.tensor_tensor(wdiff[:, :], m2[:, :], m1[:, :], ALU.subtract).then_inc(S["wdiff_ready"], 1)
                dve.wait_ge(S["pe_rank"], g)
                dve.tensor_tensor(M[:, :, :], oh1[:, :, :], oh2[:, :, :], ALU.add)
                link(dve.tensor_copy(Mpre[:, 0, :], Mpre[:, GB, :]))
                for i in range(GB):
                    ins = dve.tensor_tensor(Mpre[:, i + 1, :], Mpre[:, i, :], M[:, i, :], ALU.add)
                    if i < GB - 1:
                        link(ins)
                    else:
                        ins.then_inc(S["chosen"], 1)

            def place(g, link):
                dve.wait_ge(S["pe_rank"], g + 1)
                dve.tensor_tensor(rank[:, :, :], B_W[:, 0:GB * E].rearrange("p (b e) -> p b e", e=E),
                                  rk[:, 1:2, :].broadcast_to([P, GB, E]), ALU.add).then_inc(S["placed"], 1)
                dve.wait_ge(S["placed"], g + 1)
                dve.tensor_tensor(pick[:, 0, :, :], rank[:, :, :], oh1[:, :, :], ALU.mult)
                link(dve.tensor_tensor(pick[:, 1, :, :], rank[:, :, :], oh2[:, :, :], ALU.mult))
                link(dve.reduce_sum(slot_f[:, :, :], pick[:, :, :, :], AX_X))
                dve.tensor_copy(slot[:, :, :], slot_f[:, :, :]).then_inc(S["slot_ready"], 1)
                dve.wait_ge(S["wgt_ready"], g + 1)
                dve.tensor_copy(rows[:, :, 1, 0:P], rows[:, :, 0, 0:P])
                dve.tensor_copy(rows[:, :, :, P:P + 1].bitcast(U32).rearrange("p b k o -> p b (k o)"),
                                dst[:, bass.ds(g * GB, GB), :])
                dve.tensor_copy(rows[:, :, :, P + 1:ROW].rearrange("p b k o -> p b (k o)"),
                                wgt[:, :, :].rearrange("p k b -> p b k")).then_inc(S["rows_ready"], 1)

            def tail(g, final):
                done[0] = 0

                def glink(ins):
                    link(ins, START + g * LINKS)

                def between(e):
                    if e == 1:
                        norm_stats(g, glink)
                    if e == 3:
                        norm_apply(g, glink)
                    if e == 4:
                        residual(g)
                    if e == 6:
                        hidden(g, 0)
                    if e == 7:
                        hidden(g, 1)

                if final:
                    for e in range(1, E):
                        between(e)
                else:
                    recur(g + 1, between)
                hidden(g, 2)
                hidden(g, 3)
                route(g, glink)
                place(g, glink)
                assert done[0] == LINKS, done[0]

            recur(0, lambda e: None)
            with dve.Fori(0, NG - 1) as g:
                tail(g, False)
            tail(NG - 1, True)

            done[0] = START + NG * LINKS
            dve.wait_ge(S["pe_cnt"], 1)
            link(dve.tensor_copy(cnt[:, :], B_W[0:1, 0:E]))
            link(dve.tensor_tensor(cmp16[:, :, :], cnt[:, :].unsqueeze(2).broadcast_to([1, E, NB]),
                                   jno[0:1, 1:2, 0:NB].broadcast_to([1, E, NB]), ALU.is_gt))
            link(dve.reduce_sum(ctiles[:, :], cmp16[:, :, :], AX_X))
            link(dve.tensor_tensor_scan(cends[:, :], ones_e[:, :], ctiles[:, :], 0.0, ALU.mult, ALU.add))
            jn = jno[:, 0, :]
            link(dve.tensor_tensor(jge[:, :, :], cends[:, :].unsqueeze(1).broadcast_to([1, JOBS, E]),
                                   jn.unsqueeze(2).broadcast_to([1, JOBS, E]), ALU.is_le))
            link(dve.reduce_sum(jex[:, :], jge[:, :, :], AX_X))
            link(dve.tensor_tensor(jge[:, :, :], jge[:, :, :], ctiles[:, :].unsqueeze(1).broadcast_to([1, JOBS, E]), ALU.mult))
            link(dve.reduce_sum(jst[:, :], jge[:, :, :], AX_X))
            link(dve.tensor_tensor(jst[:, :], jn, jst[:, :], ALU.subtract))
            link(dve.tensor_scalar(jok[:, :], jex[:, :], E - 0.5, float(P), ALU.is_lt, ALU.mult))
            link(dve.tensor_tensor(jst[:, :], jst[:, :], jok[:, :], ALU.mult))
            link(dve.tensor_scalar(jtmp[:, :], jex[:, :], float(REGION), None, ALU.mult))
            link(dve.tensor_tensor(jrow[:, :], jst[:, :], jtmp[:, :], ALU.add))
            link(dve.tensor_scalar(jwex[:, :], jex[:, :], float(E - 1), None, ALU.min))
            link(dve.tensor_tensor(padf[:, :], cnt[:, :], rk[0:1, 1, :], ALU.add))
            dve.tensor_copy(padr[:, :], padf[:, :]).then_inc(S["jobs_ready"], 1)

            def job_in(j, r):
                dve.wait_ge(S["pe_jx"], j + 1)
                dve.tensor_copy(jT[:, r, :], J_X[:, 0:P]).then_inc(S["jT_ready"], 1)
                meta = jmeta[:, bass.ds(j, 1), :].rearrange("p j c -> p (j c)")
                dve.tensor_copy(meta[:, 0:1].bitcast(U32), jin[:, r, P:P + 1].bitcast(U32))
                dve.tensor_copy(meta[:, 1:2], jin[:, r, P + 1:ROW]).then_inc(S["jin_free"], 1)

            def job_tr(j, r):
                dve.wait_ge(S["pe_jt"], j + 1)
                dve.tensor_copy(actT[:, r, :], J_T[:, :]).then_inc(S["actT_ready"], 1)

            def job_out(j, r, t):
                dve.wait_ge(S["pe_jo"], j + 1)
                dve.wait_ge(s_put[r], t * 16)
                dve.wait_ge(S["jin_free"], j + 1)
                meta = jmeta[:, bass.ds(j, 1), :].rearrange("p j c -> p (j c)")
                dve.tensor_copy(jidx[:, r:r + 1], meta[:, 0:1].bitcast(U32)).then_inc(s_put_idx[r], 1)
                dve.tensor_scalar(res[:, r, :], J_O[:, 0:P], meta[:, 1:2], None, ALU.mult).then_inc(s_put_res[r], 1)

            job_in(0, 0)
            job_in(1, 1)
            job_in(2, 2)
            job_tr(0, 0)
            job_in(3, 0)
            job_tr(1, 1)
            job_out(0, 0, 0)
            with dve.Fori(0, JOBS // RING - 2) as t:
                for r in range(RING):
                    job_in(t * RING + RING + r + 1, (r + 1) % RING)
                    job_tr(t * RING + RING + r - 1, (r - 1) % RING)
                    job_out(t * RING + RING + r - 2, (r - 2) % RING, t + (1 if r == 2 else 0))
            last0 = JOBS - RING
            for j in range(last0, JOBS):
                if j + 1 < JOBS:
                    job_in(j + 1, (j + 1) % RING)
                job_tr(j - 1, (j - 1) % RING)
                job_out(j - 2, (j - 2) % RING, (j - 2) // RING)
            job_tr(JOBS - 1, (JOBS - 1) % RING)
            for j in (JOBS - 2, JOBS - 1):
                job_out(j, j % RING, j // RING)

            for g in range(NG):
                dve.wait_ge(s_y[g % 2], 32 * (g // 2 + 1))
                link(dve.tensor_tensor(y0[:, g % 2, :], y0[:, g % 2, :], y1[:, g % 2, :], ALU.add))
                dve.tensor_tensor(y0[:, g % 2, :], y0[:, g % 2, :], x1[:, g * GB:(g + 1) * GB, :].rearrange("p b d -> p (b d)"),
                                  ALU.add).then_inc(S["added"], 1)

        @block.tensor
        def _(pe):
            def w(k):
                return wr[:, k * P:(k + 1) * P]

            def project_h(g):
                pe.wait_ge(S["act_v"], g)
                pe.matmul(B_XC[:, :], wf[:, 0:P], x_sb[:, grp(g)], start=True, stop=False)
                pe.wait_ge(S["act_k"], g)
                pe.matmul(B_HK[:, :], wf[:, P:2 * P], x_sb[:, grp(g)], start=True, stop=True).then_inc(S["pe_h"], 1)

            def project_c(g):
                pe.wait_ge(S["act_hs"], g + 1)
                pe.matmul(B_XC[:, :], w(0), hs[:, :], start=False, stop=True).then_inc(S["pe_xc"], 1)

            def project_vk(g):
                pe.wait_ge(S["act_xc"], g + 1)
                pe.matmul(B_XC[:, :], w(1), xc[:, :], start=True, stop=True).then_inc(S["pe_v"], 1)
                pe.matmul(B_HK[:, :], w(2), xc[:, :], start=True, stop=True).then_inc(S["pe_k"], 1)

            def gate_q(g):
                pe.wait_ge(S["prod_ready"], g * E)
                pe.matmul(B_A[:, :], w(3), xc[:, :], start=True, stop=True).then_inc(S["pe_g"], 1)
                pe.matmul(B_Q[:, :], w(4), xc[:, :], start=True, stop=True).then_inc(S["pe_q"], 1)

            def reduce_y(g):
                pe.wait_ge(S["x1_ready"], g)
                for r in range(2):
                    pe.wait_ge(S["prod_ready"], g * E + 4 * (r + 1))
                    for j in range(4):
                        e = 4 * r + j
                        last = pe.matmul(B_Y[32 * j:32 * j + 32, :], sel[:, e, :], prod[:, e, :],
                                         start=(r == 0), stop=(r == 1))
                last.then_inc(S["pe_y"], 1)

            def up_gate(g, n):
                pe.wait_ge(S["c_ready"], g * GB + (n - 1 if n else 0))
                e = pe.value_load(cexp[0:1, bass.ds(g * GB + n, 1)], min_val=0, max_val=E - 1)
                pe.matmul(B_ROW[n % 2][:, :], x1T[:, n * P:(n + 1) * P], wug[:, bass.ds(e * (2 * H2), 2 * H2)],
                          start=True, stop=False)
                pe.matmul(B_ROW[n % 2][:, :], ones[:, :], brow[:, bass.ds(e * (2 * H2) + BUG, 2 * H2)],
                          start=False, stop=True).then_inc(S["pe_ug"], 1)
                return e

            def hidden_T(g, n):
                pe.wait_ge(S["hid_ready"], g * GB + n + 1)
                for c in range(2):
                    last = pe.transpose(B_ROW[n % 2][:, c * P:(c + 1) * P], hid[:, n % 2, c * P:(c + 1) * P], ident[:, :])
                last.then_inc(S["pe_ht"], 1)

            def down(g, n, e):
                pe.wait_ge(S["hidT_ready"], g * GB + n + 1)
                for c in range(2):
                    pe.matmul(B_ROW[n % 2][:, 0:P], hidT[:, n % 2, c * P:(c + 1) * P],
                              wd[:, bass.ds(e * (2 * P) + c * P, P)], start=(c == 0), stop=False)
                pe.matmul(B_ROW[n % 2][:, 0:P], ones[:, :], brow[:, bass.ds(e * P + BDO, P)],
                          start=False, stop=True).then_inc(S["pe_c"], 1)

            def conditional(g):
                pe.wait_ge(S["x1_ready"], g + 1)
                reg = {0: up_gate(g, 0), 1: up_gate(g, 1)}
                for n in range(0, GB, 2):
                    hidden_T(g, n)
                    hidden_T(g, n + 1)
                    down(g, n, reg[n])
                    down(g, n + 1, reg[n + 1])
                    if n + 2 < GB:
                        reg[n + 2] = up_gate(g, n + 2)
                        reg[n + 3] = up_gate(g, n + 3)
                pe.wait_ge(S["placed"], g)
                for n in range(GB):
                    pe.wait_ge(S["c_ready"], g * GB + n + 1)
                    last = pe.transpose(B_W[:, n * P:(n + 1) * P], rows[:, n, 0, 0:P], ident[:, :])
                last.then_inc(S["pe_ct"], 1)
                pe.wait_ge(S["cT_ready"], g + 1)
                for n in range(GB):
                    last = pe.matmul(B_W[:, n * E:(n + 1) * E], cT[:, n * P:(n + 1) * P], wrt[:, :],
                                     start=(n == 0), stop=(n == GB - 1), skip_group_check=True)
                last.then_inc(S["pe_l"], 1)
                pe.wait_ge(S["lg_copied"], g + 1)
                for n in range(GB):
                    last = pe.transpose(B_W[:, n * P:(n + 1) * P], x1T[:, n * P:(n + 1) * P], ident[:, :])
                last.then_inc(S["pe_x1"], 1)

            def ranks_of(g):
                pe.wait_ge(S["x1_copied"], g + 1)
                pe.wait_ge(S["chosen"], g + 1)
                pe.matmul(B_W[:, 0:GB * E], bef[:, :], M[:, :, :].rearrange("p b e -> p (b e)"), start=True, stop=False)
                pe.matmul(B_W[:, 0:GB * E], ones[:, :], Mpre[:, 0:GB, :].rearrange("p b e -> p (b e)"),
                          start=False, stop=True).then_inc(S["pe_rank"], 1)

            def tail(g, ahead, final):
                reduce_y(g)
                if not final:
                    gate_q(g + 1)
                pe.wait_ge(S["act_y"], g + 1)
                for i in range(GB):
                    last = pe.transpose(B_Y[:, i * P:(i + 1) * P], y_sb[:, i * P:(i + 1) * P], ident[:, :])
                last.then_inc(S["pe_yt"], 1)
                if ahead:
                    project_h(g + 2)
                pe.wait_ge(S["z_ready"], g + 1)
                for i in range(GB):
                    last = pe.transpose(B_Y[:, i * P:(i + 1) * P], z_sb[:, i * P:(i + 1) * P], ident[:, :])
                last.then_inc(S["pe_zt"], 1)
                pe.wait_ge(S["act_zn"], g + 1)
                pe.matmul(B_Y[:, :], w(5), zn[:, :], start=True, stop=True).then_inc(S["pe_o"], 1)
                if ahead:
                    project_c(g + 2)
                    project_vk(g + 2)
                conditional(g)
                ranks_of(g)

            pe.wait_ge(S["s_wf"], 16)
            pe.wait_ge(S["s_wr"], 16)
            pe.wait_ge(S["s_x"], 16 * NG)
            pe.wait_ge(S["s_c"], 16 * 11)
            project_h(0)
            project_c(0)
            project_vk(0)
            gate_q(0)
            project_h(1)
            project_c(1)
            project_vk(1)
            pe.wait_ge(S["s_ugd"], 16 * 2)
            pe.wait_ge(S["s_bias_rows"], 16)
            pe.wait_ge(S["expert_ready"], 1)
            pe.wait_ge(S["ones_ready"], 1)
            pe.wait_ge(S["before_ready"], 1)
            with pe.Fori(0, NG - 2) as g:
                tail(g, True, False)
            tail(NG - 2, False, False)
            tail(NG - 1, False, True)
            pe.wait_ge(S["placed"], NG)
            pe.matmul(B_W[:, 0:E], ones[:, :], Mpre[:, GB, :], start=True, stop=True).then_inc(S["pe_cnt"], 1)

            def job_in(j, r, n):
                pe.wait_ge(s_job[r], n * 16 + 16)
                pe.wait_ge(S["jT_ready"], j)
                pe.transpose(J_X[:, 0:P], jin[:, r, 0:P], ident[:, :]).then_inc(S["pe_jx"], 1)

            def expert_of(j):
                return pe.value_load(jwex[0:1, bass.ds(j, 1)], min_val=0, max_val=E - 1)

            def job_up(j, r, e):
                pe.wait_ge(S["jT_ready"], j + 1)
                if r is not None:
                    pe.wait_ge(S["gelu_done"], r[1])
                    r = r[0]
                pe.matmul(J_H[r][:, :], jT[:, r, :], w1[:, bass.ds(e * FF, FF)], start=True, stop=False)
                pe.matmul(J_H[r][:, :], ones[:, :], brow[:, bass.ds(e * FF + B1O, FF)],
                          start=False, stop=True).then_inc(S["pe_jh"], 1)

            def job_tr(j, r):
                pe.wait_ge(S["gelu_done"], j + 1)
                pe.wait_ge(S["actT_ready"], j)
                for c in range(FC):
                    last = pe.transpose(J_T[:, c * P:(c + 1) * P], act_sb[:, r, c * P:(c + 1) * P], ident[:, :])
                last.then_inc(S["pe_jt"], 1)

            def job_down(j, r, e, before):
                pe.wait_ge(S["actT_ready"], j + 1)
                pe.wait_ge(s_put_res[(r - 1) % RING], before)
                for c in range(FC):
                    pe.matmul(J_O[:, 0:P], actT[:, r, c * P:(c + 1) * P],
                              w2[:, bass.ds(e * (FC * P) + c * P, P)], start=(c == 0), stop=False)
                pe.matmul(J_O[:, 0:P], ones[:, :], brow[:, bass.ds(e * P + B2O, P)],
                          start=False, stop=True).then_inc(S["pe_jo"], 1)

            pe.wait_ge(S["s_w12"], 16 * 2)
            pe.wait_ge(S["jobs_ready"], 1)
            job_in(0, 0, 0)
            job_in(1, 1, 0)
            job_up(0, (0, 0), expert_of(0))
            job_in(2, 2, 0)
            job_up(1, (1, 0), expert_of(1))
            job_tr(0, 0)
            job_in(3, 0, 1)
            job_up(2, (2, 0), expert_of(2))
            job_tr(1, 1)
            job_down(0, 0, expert_of(0), 0)
            with pe.Fori(0, JOBS // RING - 2) as t:
                for r in range(RING):
                    j = t * RING + RING + r
                    job_in(j + 1, (r + 1) % RING, t + (1 if r < 2 else 2))
                    job_up(j, (r, t * RING + r + 1), expert_of(j))
                    job_tr(j - 1, (r - 1) % RING)
                    job_down(j - 2, (r - 2) % RING, expert_of(j - 2), t + 1)
            for j in range(JOBS - RING, JOBS):
                if j + 1 < JOBS:
                    job_in(j + 1, (j + 1) % RING, (j + 1) // RING)
                job_up(j, (j % RING, j - RING + 1), expert_of(j))
                job_tr(j - 1, (j - 1) % RING)
                job_down(j - 2, (j - 2) % RING, expert_of(j - 2), (j - 3) // RING + 1)
            job_tr(JOBS - 1, (JOBS - 1) % RING)
            for j in (JOBS - 2, JOBS - 1):
                job_down(j, j % RING, expert_of(j), (j - 1) // RING + 1)


def kernel(x, cond_8, L0_cond_W_base, L0_cond_b_base, L0_cond_As, L0_cond_Bs, L0_attn_Wq, L0_attn_Wk, L0_attn_Wv,
           L0_attn_Wg, L0_attn_Wo, L0_attn_gamma, L0_attn_beta, L0_cond2_W_up, L0_cond2_b_up, L0_cond2_W_gate,
           L0_cond2_b_gate, L0_cond2_W_down, L0_cond2_b_down, L0_ffn_router_w, L0_ffn_w1, L0_ffn_b1, L0_ffn_w2,
           L0_ffn_b2):
    import concourse.bacc as bacc
    from concourse.bass_utils import run_bass_kernel_spmd

    a = np.asarray
    at = np.arange(P)
    yrow = (at % 16) * E + 4 * (at % 32 // 16) + at // 32
    arrays = {
        "xT": a(x).transpose(2, 0, 1).reshape(P, NT),
        "w_first": np.concatenate([a(L0_cond_W_base).T, a(L0_cond_As).reshape(P, P).T], axis=1),
        "w_rest": np.concatenate([a(L0_cond_Bs).transpose(0, 2, 1).reshape(P, P), a(L0_attn_Wv).T, a(L0_attn_Wk).T,
                                  a(L0_attn_Wg).T, a(L0_attn_Wq).T, a(L0_attn_Wo).T[yrow]], axis=1),
        "w_upgate": np.concatenate([a(L0_cond2_W_up), a(L0_cond2_W_gate)], axis=1).transpose(2, 0, 1).reshape(P, -1),
        "w_down": a(L0_cond2_W_down).reshape(E, P, 2, P).transpose(3, 0, 2, 1).reshape(P, -1),
        "w_1": a(L0_ffn_w1).transpose(2, 0, 1).reshape(P, -1),
        "w_2": a(L0_ffn_w2).reshape(E, P, FC, P).transpose(3, 0, 2, 1).reshape(P, -1),
        "w_router": a(L0_ffn_router_w).T,
        "columns": np.stack([a(L0_cond_b_base), a(L0_attn_gamma)[yrow], a(L0_attn_beta)[yrow]], axis=1),
        "cond_row": a(cond_8).reshape(1, -1),
        "cond_T": a(cond_8).T,
        "biases": np.concatenate([np.concatenate([a(L0_cond2_b_up), a(L0_cond2_b_gate)], axis=1).reshape(-1),
                                  a(L0_ffn_b1).reshape(-1), a(L0_cond2_b_down).reshape(-1),
                                  a(L0_ffn_b2).reshape(-1)]).reshape(P, -1),
    }
    select = np.zeros((P, E, 32), np.float32)
    for e in range(E):
        select[at, e, 16 * (e // 4) + at // E] = 1
    arrays["identity"] = np.eye(P, dtype=np.float32)
    arrays["select"] = select.reshape(P, -1)
    arrays["before"] = np.triu(np.ones((P, P), np.float32), 1)
    arrays["ranks"] = np.tile(np.concatenate([E - np.arange(E), REGION * np.arange(E)]).astype(np.float32), (P, 1))
    arrays["dest"] = (at[:, None, None] + P * np.arange(NB)[None, :, None]
                      + NT * np.arange(TOPK)[None, None, :]).astype(np.uint32).reshape(P, -1)
    arrays["job_no"] = np.stack([np.arange(JOBS), P * np.arange(JOBS)]).astype(np.float32).reshape(1, -1)

    nc = bacc.Bacc("TRN2", target_bir_lowering=False, num_devices=1)
    arrays = {k: np.ascontiguousarray(v) for k, v in arrays.items()}
    aps = {k: nc.dram_tensor(k, list(v.shape), mybir.dt.from_np(v.dtype), kind="ExternalInput").ap()
           for k, v in arrays.items()}
    out = nc.dram_tensor("out", [NB, P, P], F32, kind="ExternalOutput").ap()
    adaln_attn_ffn_kernel(nc, out=out, **aps)
    r = run_bass_kernel_spmd(nc, [arrays], core_ids=[0])
    return r.results[0]["out"]
```

```python
from contextlib import ExitStack

import numpy as np

import concourse.bass as bass
from concourse import mybir

F32 = mybir.dt.float32
BF16 = mybir.dt.bfloat16
I32 = mybir.dt.int32
U32 = mybir.dt.uint32
ALU = mybir.AluOpType
ACT = mybir.ActivationFunctionType
AX_X = mybir.AxisListType.X

P = 128
NB = 16
E = 8
NH = 16
GB = 4
NG = NB // GB
GT = GB * P
NT = NB * P
H2 = 256
FF = 512
FC = FF // P
TOPK = 2
LN_EPS = 1e-5
LORA_SCALE = 2.0
ROW = P + 2
REGION = NT + P
DUMMY = E * REGION
JOBS = (NT * TOPK + E * (P - 1)) // P
RING = 3
NOWHERE = 1 << 20
BUG, BDO, B2O, NBIAS = 0, E * 2 * H2, E * (2 * H2 + P), E * (2 * H2 + 2 * P)
C_BEFORE = P + E * 32
C_RANKS = C_BEFORE + P
C_ROUTER = C_RANKS + 2 * E
C_COLS = C_ROUTER + E
C_BIAS = C_COLS + 3
SMALL = C_BIAS + NBIAS // P
assert JOBS % RING == 0


def adaln_attn_ffn_kernel(nc, xT, w_first, w_rest, w_upgate, w_down, w_1, w_2, small, cond_row, cond_T,
                          dest, job_no, out):
    v_rows = nc.dram_tensor("v_rows", [NG, P, GT], F32).ap()
    bias_rows = nc.dram_tensor("bias_rows", [3, NBIAS], BF16).ap()
    routed = nc.dram_tensor("routed", [DUMMY + P, ROW], F32).ap()
    mixed = nc.dram_tensor("mixed", [TOPK * NT, P], F32).ap()

    with ExitStack() as ctx:
        def sb(name, shape, dt=F32):
            return ctx.enter_context(nc.sbuf_tensor(name, shape, dt))

        def sem(name):
            return ctx.enter_context(nc.semaphore(name))

        x_sb = sb("x_sb", [P, NT])
        wf = sb("wf", [P, 2 * P])
        wr = sb("wr", [P, 6 * P])
        wug = sb("wug", [P, E * 2 * H2])
        wd = sb("wd", [P, E * 2 * P])
        w1j = sb("w1j", [P, RING, FF + FC])
        w2 = sb("w2", [P, E * FC * P])
        crow_w = sb("crow_w", [1, NB, E])
        ccol = sb("ccol", [P, NB])
        ccol2 = sb("ccol2", [P, NB])
        b_part = sb("b_part", [P, 3, NBIAS // P], BF16)
        b_rest = sb("b_rest", [P, 2, NBIAS // P])
        brow = sb("brow", [P, NBIAS], BF16)
        small_sb = sb("small_sb", [P, SMALL])
        ident = small_sb[:, 0:P]
        sel = small_sb[:, P:P + E * 32].rearrange("p (e c) -> p e c", e=E)
        bef_f = small_sb[:, C_BEFORE:C_BEFORE + P]
        rk = small_sb[:, C_RANKS:C_RANKS + 2 * E].rearrange("p (a e) -> p a e", a=2)
        wrt = small_sb[:, C_ROUTER:C_ROUTER + E]
        cols = small_sb[:, C_COLS:C_COLS + 3]
        b_in = small_sb[:, C_BIAS:SMALL]
        bef = sb("bef", [P, P], BF16)
        ones = sb("ones", [P, P], BF16)
        dst = sb("dst", [P, NB, TOPK], U32)
        jno = sb("jno", [1, 2, JOBS])
        hs = sb("hs", [P, GT])
        xc = sb("xc", [P, GT])
        v_sb = sb("v_sb", [P, GT])
        k_sb = sb("k_sb", [P, NT])
        state = sb("state", [P, 2, E, GT])
        prod = sb("prod", [P, E, GT])
        y_sb = sb("y_sb", [P, GT])
        bst = sb("bst", [P, GB, 6])
        mv = sb("mv", [P, GB, 2])
        var = sb("var", [P, GB])
        sd = sb("sd", [P, GB])
        rstd = sb("rstd", [P, GB])
        z_sb = sb("z_sb", [P, GT])
        zn = sb("zn", [P, GT])
        x1T = sb("x1T", [P, GT])
        cmax = sb("cmax", [1, NB])
        ceq = sb("ceq", [1, NB, E])
        crk = sb("crk", [1, NB])
        cexp = sb("cexp", [1, NB], I32)
        silu_sb = sb("silu_sb", [P, 2, H2])
        hid = sb("hid", [P, 2, H2])
        hidT = sb("hidT", [P, 2, H2])
        c_sb = sb("c_sb", [P, GT])
        cT = sb("cT", [P, GT])
        rows = sb("rows", [P, GB, TOPK, ROW])
        x1 = sb("x1", [P, NB, P])
        lg = sb("lg", [P, GB, E])
        lg2 = sb("lg2", [P, GB, E])
        m1 = sb("m1", [P, GB])
        m2 = sb("m2", [P, GB])
        eq = sb("eq", [P, GB, E])
        rr = sb("rr", [P, GB])
        oh1 = sb("oh1", [P, GB, E])
        oh2 = sb("oh2", [P, GB, E])
        rank = sb("rank", [P, GB, E])
        pick = sb("pick", [P, TOPK, GB, E])
        wdiff = sb("wdiff", [P, GB])
        M = sb("M", [P, GB, E], BF16)
        Mpre = sb("Mpre", [P, GB + 1, E], BF16)
        slot_f = sb("slot_f", [P, TOPK, GB])
        slot = sb("slot", [P, TOPK, GB], U32)
        cnt = sb("cnt", [1, E])
        ctiles = sb("ctiles", [1, E])
        cmp16 = sb("cmp16", [1, E, NB])
        cends = sb("cends", [1, E])
        ones_e = sb("ones_e", [1, E])
        jge = sb("jge", [1, JOBS, E])
        jex = sb("jex", [1, JOBS])
        jst = sb("jst", [1, JOBS])
        jok = sb("jok", [1, JOBS])
        jtmp = sb("jtmp", [1, JOBS])
        jrow = sb("jrow", [1, JOBS], I32)
        jwex = sb("jwex", [1, JOBS], I32)
        padf = sb("padf", [1, E])
        padr = sb("padr", [1, E], I32)
        pad = sb("pad", [P, ROW])
        late = state[:, :, :, :].rearrange("p g e t -> p (g e t)")
        at = [0]

        def carve(*shape):
            n = int(np.prod(shape))
            a = late[:, at[0]:at[0] + n]
            at[0] += n
            assert at[0] <= 2 * E * GT
            return a.rearrange({2: "p (a b) -> p a b", 3: "p (a b c) -> p a b c"}[len(shape)],
                               **dict(zip("abc", shape)))

        jin = carve(RING, ROW)
        jmeta = carve(JOBS, 2)
        jT = carve(RING, P)
        actT = carve(RING, FF)
        res = carve(RING, P)
        y0 = carve(NG, GT)
        y1 = carve(NG, GT)
        jidx = sb("jidx", [P, RING], U32)

        bank = [ctx.enter_context(nc.psum_tensor(f"bank{i}", [P, GT], F32)) for i in range(8)]
        B_XC, B_HK, B_A, B_Q, B_Y = bank[0:5]
        B_ROW, B_W = bank[5:7], bank[7]
        J_H, J_X, J_O = bank[0:3], bank[3], bank[4:7]

        names = """s_x0 s_x s_wf s_wr s_cond s_small s_crow s_late s_ugd s_w2 s_bias_out s_bias_rows s_pad s_padrow s_vst s_scatter s_out
            ones_ready brow_zero before_ready bias_split expert_ready ccol_ready
            pe_h pe_xc pe_v pe_k pe_g pe_q pe_y pe_yt pe_zt pe_o
            act_hs act_xc act_v act_k act_a act_y act_sd act_zn
            kv_ready a_zeroed scanned prod_ready dve_chain norm_chain route_chain stats_ready var_ready z_ready x1_ready
            pe_ug pe_ht pe_c pe_ct pe_l pe_x1 pe_rank pe_cnt
            silu_done hid_ready hidT_ready c_ready cT_ready x1_copied
            lg_copied wdiff_ready chosen placed rows_free slot_ready rows_ready jobs_ready
            pads_ready pe_jx pe_jh pe_jo jT_ready jin_free gelu_done added""".split()
        S = {n: sem(n) for n in names}
        s_vload = [sem(f"s_vload{e}") for e in range(E)]
        s_job = [sem(f"s_job{r}") for r in range(RING)]
        s_put_idx = [sem(f"s_put_idx{r}") for r in range(RING)]
        s_put_res = [sem(f"s_put_res{r}") for r in range(RING)]
        s_put = [sem(f"s_put{r}") for r in range(RING)]
        s_w1j = [sem(f"s_w1j{r}") for r in range(RING)]
        s_y = [sem(f"s_y{g}") for g in range(NG)]

        block = ctx.enter_context(nc.Block())

        def grp(g):
            return bass.ds(g * GT, GT)

        def pad_experts(eng, half):
            eng.wait_ge(S["pads_ready"], 1)
            with eng.Fori(half * (E // 2), (half + 1) * (E // 2)) as e:
                r = eng.value_load(padr[0:1, bass.ds(e, 1)], min_val=0, max_val=DUMMY - P)
                eng.dma_start(routed[bass.ds(r, P), :], pad[:, :]).then_inc(S["s_padrow"], 16)

        def load_results(eng, k, y):
            for r in range(RING):
                eng.wait_ge(s_put[r], 16 * (JOBS // RING))
            for g in range(NG):
                eng.dma_start(y[:, g, :], mixed[k * NT + g * GT:k * NT + (g + 1) * GT, :]
                              .rearrange("(p b) d -> p (b d)", p=P)).then_inc(s_y[g], 16)

        @block.sync
        def _(sp):
            sp.dma_start(wf[:, :], w_first).then_inc(S["s_wf"], 16)
            sp.dma_start(x_sb[:, 0:GT], xT[:, 0:GT]).then_inc(S["s_x0"], 16)
            sp.dma_start(wr[:, :], w_rest).then_inc(S["s_wr"], 16)
            sp.dma_start(x_sb[:, GT:NT], xT[:, GT:NT]).then_inc(S["s_x"], 16)
            sp.dma_start(wug[:, :], w_upgate).then_inc(S["s_ugd"], 16)
            sp.dma_start(wd[:, :], w_down).then_inc(S["s_ugd"], 16)

            def spread_v(g, used):
                sp.wait_ge(S["act_v"], g + 1)
                sp.dma_start(v_rows[bass.ds(g, 1), :, :].rearrange("g p t -> p (g t)"), v_sb[:, :]).then_inc(S["s_vst"], 16)
                sp.wait_ge(S["s_vst"], g * 16 + 16)
                for e in range(E):
                    if used is not None:
                        sp.wait_ge(S["prod_ready"], used * E + e + 1)
                    src = v_rows[bass.ds(g, 1), :, :].rearrange("g (h e) t -> (g h) e t", e=E)[:, e, :]
                    sp.dma_start(state[:, bass.ds(g % 2, 1), e, :].rearrange("p g t -> p (g t)"),
                                 src.unsqueeze(1).broadcast_to([NH, E, GT])).then_inc(s_vload[e], 16)

            spread_v(0, None)
            spread_v(1, None)
            sp.dma_start(w2[:, :], w_2).then_inc(S["s_w2"], 16)

            def rows_sent(n):
                sp.wait_ge(S["s_scatter"], n * (16 * GB * TOPK))
                sp.sem_inc(S["rows_free"], 1)

            spread_v(2, 0)
            with sp.Fori(1, NG - 2) as g:
                spread_v(g + 2, g)
                rows_sent(g)
            rows_sent(NG - 2)
            rows_sent(NG - 1)
            sp.wait_ge(S["s_pad"], 3)
            sp.dma_start(routed[DUMMY:DUMMY + P, :], pad[:, :]).then_inc(S["s_padrow"], 16)
            pad_experts(sp, 0)

            def load_weights(j, r, used):
                e = sp.value_load(jwex[0:1, bass.ds(j, 1)], min_val=0, max_val=E - 1)
                if used is not None:
                    sp.wait_ge(S["gelu_done"], used)
                sp.dma_start(w1j[:, r, :], w_1[bass.ds(e, 1), :, :].rearrange("e p f -> p (e f)")).then_inc(s_w1j[r], 16)

            def load_rows(j, r, free):
                row = sp.value_load(jrow[0:1, bass.ds(j, 1)], min_val=0, max_val=DUMMY)
                if free is not None:
                    sp.wait_ge(S["jin_free"], free)
                sp.dma_start(jin[:, r, :], routed[bass.ds(row, P), :]).then_inc(s_job[r], 16)

            sp.wait_ge(S["jobs_ready"], 1)
            for r in range(RING):
                load_weights(r, r, None)
            sp.wait_ge(S["s_padrow"], 16 * (E + 1))
            sp.wait_ge(S["s_scatter"], 16 * NB * TOPK)
            for r in range(RING):
                load_rows(r, r, None)
            with sp.Fori(0, JOBS // RING - 1) as t:
                for r in range(RING):
                    load_rows(t * RING + RING + r, r, t * RING + r + 1)
                    load_weights(t * RING + RING + r, r, t * RING + r + 1)
            load_results(sp, 0, y0)
            for g in range(NG):
                sp.wait_ge(S["added"], g + 1)
                sp.dma_start(out[g * GB:(g + 1) * GB].rearrange("b p d -> p b d"),
                             y0[:, g, :].rearrange("p (b d) -> p b d", d=P)).then_inc(S["s_out"], 16)
            sp.wait_ge(S["s_out"], 16 * NG)

        @block.gpsimd
        def _(pool):
            pool.memset(ones[:, :], 1.0).then_inc(S["ones_ready"], 1)
            pool.memset(pad[:, 0:P], 0.0).then_inc(S["s_pad"], 1)
            pool.memset(pad[:, P:P + 1].bitcast(U32), NOWHERE).then_inc(S["s_pad"], 1)
            pool.memset(pad[:, P + 1:ROW], 0.0).then_inc(S["s_pad"], 1)
            pool.memset(brow[:, :].bitcast(U32), 0).then_inc(S["brow_zero"], 1)
            pool.wait_ge(S["bias_split"], 3)
            pool.dma_start(bias_rows.rearrange("k (p n) -> p k n", p=P), b_part[:, :, :]).then_inc(S["s_bias_out"], 16)

            def key_value(g):
                half = g % 2 if isinstance(g, int) else pool.snap(g % 2)
                pool.wait_ge(S["act_k"], g + 1)
                for e in range(E):
                    pool.wait_ge(s_vload[e], g * 16 + 16)
                    st = state[:, bass.ds(half, 1), e, :].rearrange("p g t -> p (g t)")
                    pool.tensor_tensor(st, st, k_sb[:, grp(g)], ALU.mult).then_inc(S["kv_ready"], 1)

            def scatter(groups):
                pool.wait_ge(S["brow_zero"], 1)
                pool.wait_ge(S["slot_ready"], groups)
                pool.wait_ge(S["rows_ready"], groups)
                for i in range(GB):
                    for k in range(TOPK):
                        pool.indirect_dma_start(
                            out=routed, out_offset=bass.IndirectOffsetOnAxis(ap=slot[:, k, i:i + 1], axis=0),
                            in_=rows[:, i, k, :], in_offset=None,
                            bounds_check=DUMMY - 1, oob_is_err=False).then_inc(S["s_scatter"], 16)

            pool.wait_ge(S["s_bias_out"], 16)
            pool.wait_ge(S["brow_zero"], 1)
            pool.dma_start(brow[0:3, :], bias_rows).then_inc(S["s_bias_rows"], 16)
            for g in range(3):
                key_value(g)
            with pool.Fori(1, NG - 2) as g:
                key_value(g + 2)
                scatter(g)
            for n in range(NG - 2, NG + 1):
                scatter(n)
            with pool.Fori(1, JOBS // RING + 1) as n:
                for r in range(RING):
                    pool.wait_ge(S["brow_zero"], 1)
                    pool.wait_ge(s_put_idx[r], n)
                    pool.wait_ge(s_put_res[r], n)
                    pool.indirect_dma_start(
                        out=mixed, out_offset=bass.IndirectOffsetOnAxis(ap=jidx[:, r:r + 1], axis=0),
                        in_=res[:, r, :], in_offset=None,
                        bounds_check=TOPK * NT - 1, oob_is_err=False).then_inc(s_put[r], 16)

        @block.scalar
        def _(act):
            act.dma_start(ccol[:, :], cond_T.unsqueeze(1).broadcast_to([E, NH, NB])).then_inc(S["s_cond"], 16)
            act.dma_start(small_sb[:, :], small).then_inc(S["s_small"], 16)
            act.dma_start(crow_w[:, :, :].rearrange("p b e -> p (b e)"), cond_row).then_inc(S["s_crow"], 16)
            act.dma_start(dst[:, :, :].rearrange("p b k -> p (b k)"), dest).then_inc(S["s_late"], 16)
            act.dma_start(jno[:, :, :].rearrange("p j e -> p (j e)"), job_no).then_inc(S["s_late"], 16)
            act.wait_ge(S["s_cond"], 16)
            act.activation(ccol2[:, :], ccol[:, :], ACT.Copy, scale=LORA_SCALE).then_inc(S["ccol_ready"], 1)
            act.wait_ge(S["ccol_ready"], 1)
            act.wait_ge(S["s_small"], 16)

            def take_h(g):
                act.wait_ge(S["pe_h"], g + 1)
                for i in range(GB):
                    last = act.activation(hs[:, i * P:(i + 1) * P], B_HK[:, i * P:(i + 1) * P], ACT.Copy,
                                          scale=ccol2[:, bass.ds(g * GB + i, 1)])
                last.then_inc(S["act_hs"], 1)

            def take_xc(g):
                act.wait_ge(S["pe_xc"], g + 1)
                act.wait_ge(S["pe_q"], g)
                act.activation(xc[:, :], B_XC[:, :], ACT.Identity, bias=cols[:, 0:1]).then_inc(S["act_xc"], 1)

            def take_vk(g):
                act.wait_ge(S["pe_v"], g + 1)
                act.wait_ge(S["s_vst"], g * 16)
                act.activation(v_sb[:, :], B_XC[:, :], ACT.Copy).then_inc(S["act_v"], 1)
                act.wait_ge(S["pe_k"], g + 1)
                act.activation(k_sb[:, grp(g)], B_HK[:, :], ACT.Copy).then_inc(S["act_k"], 1)

            def gate(g):
                act.wait_ge(S["pe_g"], g + 1)
                act.activation(B_A[:, :], B_A[:, :], ACT.Sigmoid).then_inc(S["act_a"], 1)

            def take_y(g):
                act.wait_ge(S["pe_y"], g + 1)
                act.activation(y_sb[:, :], B_Y[:, :], ACT.Copy).then_inc(S["act_y"], 1)

            def root(g):
                act.wait_ge(S["var_ready"], g + 1)
                act.activation(sd[:, :], var[:, :], ACT.Sqrt).then_inc(S["act_sd"], 1)

            def take_z(g):
                act.wait_ge(S["pe_zt"], g + 1)
                act.activation(zn[:, :], B_Y[:, :], ACT.Identity, bias=cols[:, 2:3], scale=cols[:, 1:2]).then_inc(S["act_zn"], 1)

            def silu(g, n):
                act.wait_ge(S["pe_ug"], g * GB + n + 1)
                act.activation(silu_sb[:, n % 2, :], B_ROW[n % 2][:, 0:H2], ACT.Silu).then_inc(S["silu_done"], 1)

            def take_hidT(g, n):
                act.wait_ge(S["pe_ht"], g * GB + n + 1)
                act.activation(hidT[:, n % 2, :], B_ROW[n % 2][:, 0:H2], ACT.Copy).then_inc(S["hidT_ready"], 1)

            def take_c(g, n):
                act.wait_ge(S["pe_c"], g * GB + n + 1)
                act.activation(c_sb[:, n * P:(n + 1) * P], B_ROW[n % 2][:, 0:P], ACT.Copy).then_inc(S["c_ready"], 1)

            def take_cT(g):
                act.wait_ge(S["pe_ct"], g + 1)
                act.activation(cT[:, :], B_W[:, :], ACT.Copy).then_inc(S["cT_ready"], 1)

            def take_x1(g):
                act.wait_ge(S["pe_x1"], g + 1)
                act.activation(x1[:, bass.ds(g * GB, GB), :].rearrange("p b d -> p (b d)"),
                               B_Y[:, :], ACT.Copy).then_inc(S["x1_copied"], 1)

            def row_values(g):
                act.wait_ge(S["c_ready"], g * GB + GB)
                act.wait_ge(S["rows_free"], g + 1)
                for k in range(TOPK):
                    act.activation(rows[:, :, k, 0:P], c_sb[:, :].rearrange("p (b d) -> p b d", d=P), ACT.Copy)

            def row_weights(g):
                act.wait_ge(S["wdiff_ready"], g + 1)
                for k in range(TOPK):
                    last = act.activation(rows[:, :, k, P + 1:ROW].rearrange("p b o -> p (b o)"), wdiff[:, :],
                                          ACT.Sigmoid, scale=1.0 if k == 1 else -1.0)
                last.then_inc(S["rows_ready"], 1)

            def step(g, first, recurs, ahead):
                if recurs:
                    gate(g + 1)
                take_y(g)
                if not first:
                    for n in range(2, GB):
                        take_hidT(g - 1, n)
                if ahead:
                    take_h(g + 2)
                if not first:
                    for n in range(2, GB):
                        take_c(g - 1, n)
                root(g)
                if not first:
                    take_cT(g - 1)
                if ahead:
                    take_xc(g + 2)
                take_z(g)
                if ahead:
                    take_vk(g + 2)
                silu(g, 0)
                silu(g, 1)
                take_x1(g)
                if not first:
                    row_values(g - 1)
                for n in range(2):
                    take_hidT(g, n)
                for n in range(2):
                    take_c(g, n)
                silu(g, 2)
                silu(g, 3)
                if not first:
                    row_weights(g - 1)

            act.sem_inc(S["rows_free"], 1)
            take_h(0)
            take_xc(0)
            take_vk(0)
            gate(0)
            take_h(1)
            take_xc(1)
            take_vk(1)
            step(0, True, True, True)
            with act.Fori(1, NG - 2) as g:
                step(g, False, True, True)
            step(NG - 2, False, True, False)
            step(NG - 1, False, False, False)
            for n in range(2, GB):
                take_hidT(NG - 1, n)
            for n in range(2, GB):
                take_c(NG - 1, n)
            take_cT(NG - 1)
            row_values(NG - 1)
            row_weights(NG - 1)
            act.wait_ge(S["s_pad"], 3)
            pad_experts(act, 1)

            def gelu(j, r, used):
                act.wait_ge(S["pe_jh"], j + 1)
                if used is not None:
                    act.wait_ge(S["pe_jo"], used)
                for c in range(FC):
                    last = act.activation(actT[:, r, c * P:(c + 1) * P], J_H[r][:, c * P:(c + 1) * P], ACT.Gelu,
                                          bias=w1j[:, r, FF + c:FF + c + 1])
                last.then_inc(S["gelu_done"], 1)

            for r in range(RING):
                gelu(r, r, None)
            with act.Fori(1, JOBS // RING) as t:
                for r in range(RING):
                    gelu(t * RING + r, r, t * RING + r - 2)
            load_results(act, 1, y1)

        @block.vector
        def _(dve):
            def chain(name, base):
                done = [base]

                def link(ins):
                    done[0] = done[0] + 1
                    ins.then_inc(S[name], 1)
                    dve.wait_ge(S[name], done[0])
                return link

            link = chain("dve_chain", 0)
            dve.wait_ge(S["s_small"], 16)
            dve.wait_ge(S["s_crow"], 16)
            link(dve.reduce_max(cmax[:, :], crow_w[:, :, :], AX_X))
            link(dve.tensor_tensor(ceq[:, :, :], crow_w[:, :, :], cmax[:, :].unsqueeze(2).broadcast_to([1, NB, E]), ALU.is_equal))
            link(dve.tensor_tensor(ceq[:, :, :], ceq[:, :, :], rk[0:1, 0:1, :].broadcast_to([1, NB, E]), ALU.mult))
            link(dve.reduce_max(crk[:, :], ceq[:, :, :], AX_X))
            dve.tensor_scalar(cexp[:, :], crk[:, :], -1.0, float(E), ALU.mult, ALU.add).then_inc(S["expert_ready"], 1)
            dve.tensor_copy(b_part[:, 0, :], b_in[:, :]).then_inc(S["bias_split"], 1)
            dve.wait_ge(S["bias_split"], 1)
            link(dve.tensor_tensor(b_rest[:, 0, :], b_in[:, :], b_part[:, 0, :], ALU.subtract))
            dve.tensor_copy(b_part[:, 1, :], b_rest[:, 0, :]).then_inc(S["bias_split"], 1)
            dve.wait_ge(S["bias_split"], 2)
            link(dve.tensor_tensor(b_rest[:, 1, :], b_rest[:, 0, :], b_part[:, 1, :], ALU.subtract))
            dve.tensor_copy(b_part[:, 2, :], b_rest[:, 1, :]).then_inc(S["bias_split"], 1)
            dve.tensor_copy(bef[:, :], bef_f[:, :]).then_inc(S["before_ready"], 1)
            link(dve.memset(ones_e[:, :], 1.0))
            link(dve.memset(Mpre[:, GB, :], 0.0))
            def unit(g, product, e):
                st = state[:, bass.ds(g % 2, 1), e, :].rearrange("p g t -> p (g t)")
                if not product:
                    dve.wait_ge(S["kv_ready"], g * E + e + 1)
                    dve.tensor_tensor_scan(st, B_A[:, :], st, 0.0, ALU.mult, ALU.add).then_inc(S["scanned"], 1)
                else:
                    dve.wait_ge(S["scanned"], g * E + e + 1)
                    if e == 0:
                        dve.wait_ge(S["pe_y"], g)
                    dve.tensor_tensor(prod[:, e, :], st, B_Q[:, :], ALU.mult).then_inc(S["prod_ready"], 1)

            def start_states(g):
                dve.wait_ge(S["act_a"], g + 1)
                dve.memset(B_A[:, :].rearrange("p (b t) -> p b t", t=P)[:, :, 0:1], 0.0).then_inc(S["a_zeroed"], 1)
                dve.wait_ge(S["a_zeroed"], g + 1)
                unit(g, False, 0)
                dve.wait_ge(S["pe_q"], g + 1)

            def units(g, lo, hi):
                for e in range(lo, hi):
                    if e < E:
                        unit(g, False, e)
                    unit(g, True, e - 1)

            NORM_LINKS, ROUTE_LINKS = 2, 17

            def norm_stats(g, link):
                dve.wait_ge(S["pe_yt"], g + 1)
                for i in range(GB):
                    last = dve.bn_stats(bst[:, i, :], B_Y[:, i * P:(i + 1) * P])
                last.then_inc(S["stats_ready"], 1)
                n_stats = g + 1 if isinstance(g, int) else dve.snap(g + 1)
                dve.wait_ge(S["s_small"], 16)
                dve.wait_ge(S["stats_ready"], n_stats)
                for i in range(GB):
                    last = dve.bn_aggr(mv[:, i, :], bst[:, i, :])
                link(last)
                dve.tensor_scalar(var[:, :], mv[:, :, 1], LN_EPS, None, ALU.add).then_inc(S["var_ready"], 1)

            def norm_apply(g, link):
                dve.wait_ge(S["act_sd"], g + 1)
                link(dve.reciprocal(rstd[:, :], sd[:, :]))
                for i in range(GB):
                    last = dve.tensor_scalar(z_sb[:, i * P:(i + 1) * P], B_Y[:, i * P:(i + 1) * P],
                                             mv[:, i, 0:1], rstd[:, i:i + 1], ALU.subtract, ALU.mult)
                last.then_inc(S["z_ready"], 1)

            def residual(g):
                dve.wait_ge(S["pe_o"], g + 1)
                dve.tensor_tensor(x1T[:, :], x_sb[:, grp(g)], B_Y[:, :], ALU.add).then_inc(S["x1_ready"], 1)

            def hidden(g, n):
                dve.wait_ge(S["silu_done"], g * GB + n + 1)
                dve.tensor_tensor(hid[:, n % 2, :], silu_sb[:, n % 2, :], B_ROW[n % 2][:, H2:2 * H2],
                                  ALU.mult).then_inc(S["hid_ready"], 1)

            def spread(ap):
                return ap.unsqueeze(2).broadcast_to([P, GB, E])

            def route(g, link):
                dve.wait_ge(S["pe_l"], g + 1)
                dve.tensor_copy(lg[:, :, :].rearrange("p b e -> p (b e)"), B_W[:, 0:GB * E]).then_inc(S["lg_copied"], 1)
                dve.wait_ge(S["lg_copied"], g + 1)
                for scores, most, onehot in ((lg, m1, oh1), (lg2, m2, oh2)):
                    link(dve.reduce_max(most[:, :], scores[:, :, :], AX_X))
                    link(dve.tensor_tensor(eq[:, :, :], scores[:, :, :], spread(most[:, :]), ALU.is_equal))
                    link(dve.tensor_tensor(eq[:, :, :], eq[:, :, :], rk[:, 0:1, :].broadcast_to([P, GB, E]), ALU.mult))
                    link(dve.reduce_max(rr[:, :], eq[:, :, :], AX_X))
                    link(dve.tensor_tensor(onehot[:, :, :], rk[:, 0:1, :].broadcast_to([P, GB, E]), spread(rr[:, :]), ALU.is_equal))
                    if scores is lg:
                        link(dve.scalar_tensor_tensor(lg2[:, :, :].rearrange("p b e -> p (b e)"),
                                                      oh1[:, :, :].rearrange("p b e -> p (b e)"), -3.0e38,
                                                      lg[:, :, :].rearrange("p b e -> p (b e)"), ALU.mult, ALU.add))

            def choose(g, link):
                dve.tensor_tensor(wdiff[:, :], m2[:, :], m1[:, :], ALU.subtract).then_inc(S["wdiff_ready"], 1)
                dve.tensor_tensor(M[:, :, :], oh1[:, :, :], oh2[:, :, :], ALU.add)
                link(dve.tensor_copy(Mpre[:, 0, :], Mpre[:, GB, :]))
                for i in range(GB):
                    ins = dve.tensor_tensor(Mpre[:, i + 1, :], Mpre[:, i, :], M[:, i, :], ALU.add)
                    if i < GB - 1:
                        link(ins)
                    else:
                        ins.then_inc(S["chosen"], 1)

            def place(g, link):
                dve.wait_ge(S["pe_rank"], g + 1)
                dve.tensor_tensor(rank[:, :, :], B_W[:, 0:GB * E].rearrange("p (b e) -> p b e", e=E),
                                  rk[:, 1:2, :].broadcast_to([P, GB, E]), ALU.add).then_inc(S["placed"], 1)
                dve.wait_ge(S["placed"], g + 1)
                dve.tensor_tensor(pick[:, 0, :, :], rank[:, :, :], oh1[:, :, :], ALU.mult)
                link(dve.tensor_tensor(pick[:, 1, :, :], rank[:, :, :], oh2[:, :, :], ALU.mult))
                link(dve.reduce_sum(slot_f[:, :, :], pick[:, :, :, :], AX_X))
                dve.wait_ge(S["rows_free"], g + 1)
                dve.tensor_copy(rows[:, :, :, P:P + 1].bitcast(U32).rearrange("p b k o -> p b (k o)"),
                                dst[:, bass.ds(g * GB, GB), :])
                dve.tensor_copy(slot[:, :, :], slot_f[:, :, :]).then_inc(S["slot_ready"], 1)

            def step(g, first, recurs):
                norm_link = chain("norm_chain", g * NORM_LINKS)
                route_link = chain("route_chain", (g - 1) * ROUTE_LINKS)
                if not first:
                    hidden(g - 1, 2)
                    hidden(g - 1, 3)
                if recurs:
                    start_states(g + 1)
                    units(g + 1, 1, 3)
                norm_stats(g, norm_link)
                if recurs:
                    units(g + 1, 3, 4)
                norm_apply(g, norm_link)
                if recurs:
                    units(g + 1, 4, 5)
                residual(g)
                if not first:
                    route(g - 1, route_link)
                hidden(g, 0)
                if not first:
                    choose(g - 1, route_link)
                hidden(g, 1)
                if recurs:
                    units(g + 1, 5, 7)
                if not first:
                    place(g - 1, route_link)
                if recurs:
                    units(g + 1, 7, E + 1)

            start_states(0)
            units(0, 1, E + 1)
            dve.wait_ge(S["s_late"], 32)
            step(0, True, True)
            with dve.Fori(1, NG - 1) as g:
                step(g, False, True)
            step(NG - 1, False, False)
            route_link = chain("route_chain", (NG - 1) * ROUTE_LINKS)
            hidden(NG - 1, 2)
            hidden(NG - 1, 3)
            route(NG - 1, route_link)
            choose(NG - 1, route_link)
            place(NG - 1, route_link)

            dve.wait_ge(S["pe_cnt"], 1)
            link(dve.tensor_copy(cnt[:, :], B_W[0:1, 0:E]))
            link(dve.tensor_tensor(padf[:, :], cnt[:, :], rk[0:1, 1, :], ALU.add))
            dve.tensor_copy(padr[:, :], padf[:, :]).then_inc(S["pads_ready"], 1)
            link(dve.tensor_tensor(cmp16[:, :, :], cnt[:, :].unsqueeze(2).broadcast_to([1, E, NB]),
                                   jno[0:1, 1:2, 0:NB].broadcast_to([1, E, NB]), ALU.is_gt))
            link(dve.reduce_sum(ctiles[:, :], cmp16[:, :, :], AX_X))
            link(dve.tensor_tensor_scan(cends[:, :], ones_e[:, :], ctiles[:, :], 0.0, ALU.mult, ALU.add))
            jn = jno[:, 0, :]
            link(dve.tensor_tensor(jge[:, :, :], cends[:, :].unsqueeze(1).broadcast_to([1, JOBS, E]),
                                   jn.unsqueeze(2).broadcast_to([1, JOBS, E]), ALU.is_le))
            link(dve.reduce_sum(jex[:, :], jge[:, :, :], AX_X))
            link(dve.tensor_tensor(jge[:, :, :], jge[:, :, :], ctiles[:, :].unsqueeze(1).broadcast_to([1, JOBS, E]), ALU.mult))
            link(dve.reduce_sum(jst[:, :], jge[:, :, :], AX_X))
            link(dve.tensor_tensor(jst[:, :], jn, jst[:, :], ALU.subtract))
            link(dve.tensor_scalar(jok[:, :], jex[:, :], E - 0.5, float(P), ALU.is_lt, ALU.mult))
            link(dve.tensor_tensor(jst[:, :], jst[:, :], jok[:, :], ALU.mult))
            link(dve.tensor_scalar(jtmp[:, :], jex[:, :], float(REGION), None, ALU.mult))
            link(dve.tensor_tensor(jrow[:, :], jst[:, :], jtmp[:, :], ALU.add))
            dve.tensor_scalar(jwex[:, :], jex[:, :], float(E - 1), None, ALU.min).then_inc(S["jobs_ready"], 1)

            def job_in(j, r):
                dve.wait_ge(S["pe_jx"], j + 1)
                dve.tensor_copy(jT[:, r, :], J_X[:, 0:P]).then_inc(S["jT_ready"], 1)
                meta = jmeta[:, bass.ds(j, 1), :].rearrange("p j c -> p (j c)")
                dve.tensor_copy(meta[:, 0:1].bitcast(U32), jin[:, r, P:P + 1].bitcast(U32))
                dve.tensor_copy(meta[:, 1:2], jin[:, r, P + 1:ROW]).then_inc(S["jin_free"], 1)

            def job_out(j, r, t):
                dve.wait_ge(S["pe_jo"], j + 1)
                if not (isinstance(t, int) and t == 0):
                    dve.wait_ge(s_put[r], t * 16)
                dve.wait_ge(S["jin_free"], j + 1)
                meta = jmeta[:, bass.ds(j, 1), :].rearrange("p j c -> p (j c)")
                dve.tensor_copy(jidx[:, r:r + 1], meta[:, 0:1].bitcast(U32)).then_inc(s_put_idx[r], 1)
                dve.tensor_scalar(res[:, r, :], J_O[r][:, 0:P], meta[:, 1:2], None, ALU.mult).then_inc(s_put_res[r], 1)

            job_in(0, 0)
            for j in range(2 * RING):
                job_in(j + 1, (j + 1) % RING)
                if j >= 2:
                    job_out(j - 2, (j - 2) % RING, (j - 2) // RING)
            with dve.Fori(2, JOBS // RING - 1) as t:
                for r in range(RING):
                    job_in(t * RING + r + 1, (r + 1) % RING)
                    job_out(t * RING + r - 2, (r - 2) % RING, t if r == 2 else t - 1)
            for j in range(JOBS - RING, JOBS + 2):
                if j + 1 < JOBS:
                    job_in(j + 1, (j + 1) % RING)
                job_out(j - 2, (j - 2) % RING, (j - 2) // RING)

            for g in range(NG):
                dve.wait_ge(s_y[g], 32)
                link(dve.tensor_tensor(y0[:, g, :], y0[:, g, :], y1[:, g, :], ALU.add))
                dve.tensor_tensor(y0[:, g, :], y0[:, g, :], x1[:, g * GB:(g + 1) * GB, :].rearrange("p b d -> p (b d)"),
                                  ALU.add).then_inc(S["added"], 1)

        @block.tensor
        def _(pe):
            def w(k):
                return wr[:, k * P:(k + 1) * P]

            def project_h(g):
                pe.wait_ge(S["act_k"], g)
                pe.wait_ge(S["act_v"], g)
                pe.matmul(B_HK[:, :], wf[:, P:2 * P], x_sb[:, grp(g)], start=True, stop=True).then_inc(S["pe_h"], 1)
                pe.matmul(B_XC[:, :], wf[:, 0:P], x_sb[:, grp(g)], start=True, stop=False)

            def project_c(g):
                pe.wait_ge(S["act_hs"], g + 1)
                pe.matmul(B_XC[:, :], w(0), hs[:, :], start=False, stop=True).then_inc(S["pe_xc"], 1)

            def project_vk(g, which):
                if which == 0:
                    pe.wait_ge(S["act_xc"], g + 1)
                    pe.matmul(B_XC[:, :], w(1), xc[:, :], start=True, stop=True).then_inc(S["pe_v"], 1)
                else:
                    pe.matmul(B_HK[:, :], w(2), xc[:, :], start=True, stop=True).then_inc(S["pe_k"], 1)

            def gate_q(g):
                pe.wait_ge(S["prod_ready"], g * E)
                pe.matmul(B_A[:, :], w(3), xc[:, :], start=True, stop=True).then_inc(S["pe_g"], 1)
                pe.matmul(B_Q[:, :], w(4), xc[:, :], start=True, stop=True).then_inc(S["pe_q"], 1)

            def reduce_y(g, first):
                if not first:
                    pe.wait_ge(S["x1_copied"], g)
                for r in range(2):
                    pe.wait_ge(S["prod_ready"], g * E + 4 * (r + 1))
                    for j in range(4):
                        e = 4 * r + j
                        last = pe.matmul(B_Y[32 * j:32 * j + 32, :], sel[:, e, :], prod[:, e, :],
                                         start=(r == 0), stop=(r == 1))
                last.then_inc(S["pe_y"], 1)

            def up_gate(g, n):
                if n >= 2:
                    pe.wait_ge(S["c_ready"], g * GB + n - 1)
                e = pe.value_load(cexp[0:1, bass.ds(g * GB + n, 1)], min_val=0, max_val=E - 1)
                pe.matmul(B_ROW[n % 2][:, :], x1T[:, n * P:(n + 1) * P], wug[:, bass.ds(e * (2 * H2), 2 * H2)],
                          start=True, stop=False)
                pe.matmul(B_ROW[n % 2][:, :], ones[:, :], brow[:, bass.ds(e * (2 * H2) + BUG, 2 * H2)],
                          start=False, stop=True).then_inc(S["pe_ug"], 1)
                return e

            def hidden_T(g, n):
                pe.wait_ge(S["hid_ready"], g * GB + n + 1)
                for c in range(2):
                    last = pe.transpose(B_ROW[n % 2][:, c * P:(c + 1) * P], hid[:, n % 2, c * P:(c + 1) * P], ident)
                last.then_inc(S["pe_ht"], 1)

            def down(g, n, e):
                pe.wait_ge(S["hidT_ready"], g * GB + n + 1)
                for c in range(2):
                    pe.matmul(B_ROW[n % 2][:, 0:P], hidT[:, n % 2, c * P:(c + 1) * P],
                              wd[:, bass.ds(e * (2 * P) + c * P, P)], start=(c == 0), stop=False)
                pe.matmul(B_ROW[n % 2][:, 0:P], ones[:, :], brow[:, bass.ds(e * P + BDO, P)],
                          start=False, stop=True).then_inc(S["pe_c"], 1)

            def c_T(g):
                for n in range(GB):
                    pe.wait_ge(S["c_ready"], g * GB + n + 1)
                    last = pe.transpose(B_W[:, n * P:(n + 1) * P], c_sb[:, n * P:(n + 1) * P], ident)
                last.then_inc(S["pe_ct"], 1)

            def logits(g):
                pe.wait_ge(S["cT_ready"], g + 1)
                for n in range(GB):
                    last = pe.matmul(B_W[:, n * E:(n + 1) * E], cT[:, n * P:(n + 1) * P], wrt[:, :],
                                     start=(n == 0), stop=(n == GB - 1), skip_group_check=True)
                last.then_inc(S["pe_l"], 1)

            def x1_rows(g):
                for n in range(GB):
                    last = pe.transpose(B_Y[:, n * P:(n + 1) * P], x1T[:, n * P:(n + 1) * P], ident)
                last.then_inc(S["pe_x1"], 1)

            def ranks_of(g):
                pe.wait_ge(S["lg_copied"], g + 1)
                pe.wait_ge(S["chosen"], g + 1)
                pe.matmul(B_W[:, 0:GB * E], bef[:, :], M[:, :, :].rearrange("p b e -> p (b e)"), start=True, stop=False)
                pe.matmul(B_W[:, 0:GB * E], ones[:, :], Mpre[:, 0:GB, :].rearrange("p b e -> p (b e)"),
                          start=False, stop=True).then_inc(S["pe_rank"], 1)

            def y_T(g):
                pe.wait_ge(S["act_y"], g + 1)
                for i in range(GB):
                    last = pe.transpose(B_Y[:, i * P:(i + 1) * P], y_sb[:, i * P:(i + 1) * P], ident)
                last.then_inc(S["pe_yt"], 1)

            def z_T(g):
                pe.wait_ge(S["z_ready"], g + 1)
                for i in range(GB):
                    last = pe.transpose(B_Y[:, i * P:(i + 1) * P], z_sb[:, i * P:(i + 1) * P], ident)
                last.then_inc(S["pe_zt"], 1)

            def mix_heads(g):
                pe.wait_ge(S["act_zn"], g + 1)
                pe.matmul(B_Y[:, :], w(5), zn[:, :], start=True, stop=True).then_inc(S["pe_o"], 1)

            def step(g, first, recurs, ahead, late):
                if recurs:
                    gate_q(g + 1)
                reduce_y(g, first)
                if not first:
                    hidden_T(g - 1, 2)
                    hidden_T(g - 1, 3)
                if ahead:
                    project_h(g + 2)
                y_T(g)
                if not first:
                    down(g - 1, 2, late[2])
                    down(g - 1, 3, late[3])
                if not first:
                    c_T(g - 1)
                if ahead:
                    project_c(g + 2)
                if not first:
                    logits(g - 1)
                z_T(g)
                if ahead:
                    project_vk(g + 2, 0)
                mix_heads(g)
                if ahead:
                    project_vk(g + 2, 1)
                pe.wait_ge(S["x1_ready"], g + 1)
                reg = [up_gate(g, n) for n in range(2)]
                x1_rows(g)
                if not first:
                    ranks_of(g - 1)
                for n in range(2):
                    hidden_T(g, n)
                for n in range(2):
                    down(g, n, reg[n])
                for n in range(2, GB):
                    up_gate(g, n)

            pe.wait_ge(S["s_wf"], 16)
            pe.wait_ge(S["s_x0"], 16)
            project_h(0)
            pe.wait_ge(S["s_wr"], 16)
            project_c(0)
            project_vk(0, 0)
            project_vk(0, 1)
            gate_q(0)
            pe.wait_ge(S["s_x"], 16)
            project_h(1)
            project_c(1)
            project_vk(1, 0)
            project_vk(1, 1)
            pe.wait_ge(S["s_small"], 16)
            pe.wait_ge(S["s_ugd"], 16 * 2)
            pe.wait_ge(S["s_bias_rows"], 16)
            pe.wait_ge(S["expert_ready"], 1)
            pe.wait_ge(S["ones_ready"], 1)
            pe.wait_ge(S["before_ready"], 1)
            def late_experts(g):
                return {n: pe.value_load(cexp[0:1, bass.ds(g * GB + n, 1)], min_val=0, max_val=E - 1) for n in (2, 3)}

            step(0, True, True, True, None)
            with pe.Fori(1, NG - 2) as g:
                step(g, False, True, True, late_experts(g - 1))
            step(NG - 2, False, True, False, late_experts(NG - 3))
            step(NG - 1, False, False, False, late_experts(NG - 2))
            late = late_experts(NG - 1)
            for n in range(2, GB):
                hidden_T(NG - 1, n)
            for n in range(2, GB):
                down(NG - 1, n, late[n])
            c_T(NG - 1)
            logits(NG - 1)
            ranks_of(NG - 1)
            pe.wait_ge(S["placed"], NG)
            pe.matmul(B_W[:, 0:E], ones[:, :], Mpre[:, GB, :], start=True, stop=True).then_inc(S["pe_cnt"], 1)

            def job_in(j, r, n):
                pe.wait_ge(s_job[r], n * 16 + 16)
                if not (isinstance(j, int) and j == 0):
                    pe.wait_ge(S["jT_ready"], j)
                pe.transpose(J_X[:, 0:P], jin[:, r, 0:P], ident).then_inc(S["pe_jx"], 1)

            def expert_of(j):
                return pe.value_load(jwex[0:1, bass.ds(j, 1)], min_val=0, max_val=E - 1)

            def job_up(j, r, n, before):
                pe.wait_ge(s_w1j[r], n * 16 + 16)
                pe.wait_ge(S["jT_ready"], j + 1)
                if before is not None:
                    pe.wait_ge(S["gelu_done"], before)
                for c in range(FC):
                    last = pe.matmul(J_H[r][:, c * P:(c + 1) * P], w1j[:, r, c * P:(c + 1) * P], jT[:, r, :],
                                     start=(c == 0), stop=(c == FC - 1), skip_group_check=True)
                last.then_inc(S["pe_jh"], 1)

            def job_down(j, r, e, before):
                pe.wait_ge(S["gelu_done"], j + 1)
                if before is not None:
                    pe.wait_ge(s_put_res[r], before)
                for c in range(FC):
                    pe.matmul(J_O[r][:, 0:P], actT[:, r, c * P:(c + 1) * P],
                              w2[:, bass.ds(e * (FC * P) + c * P, P)], start=(c == 0), stop=False)
                pe.matmul(J_O[r][:, 0:P], ones[:, :], brow[:, bass.ds(e * P + B2O, P)],
                          start=False, stop=True).then_inc(S["pe_jo"], 1)

            pe.wait_ge(S["s_w2"], 16)
            pe.wait_ge(S["jobs_ready"], 1)
            job_in(0, 0, 0)
            for j in range(RING + 2):
                job_in(j + 1, (j + 1) % RING, (j + 1) // RING)
                job_up(j, j % RING, j // RING, j - 2 if j >= RING else None)
                if j >= 2:
                    job_down(j - 2, j - 2, expert_of(j - 2), None)
            for j in range(RING + 2, 2 * RING):
                job_in(j + 1, (j + 1) % RING, (j + 1) // RING)
                job_up(j, j % RING, j // RING, j - 2)
                job_down(j - 2, (j - 2) % RING, expert_of(j - 2), 1)
            with pe.Fori(2, JOBS // RING - 1) as t:
                for r in range(RING):
                    j = t * RING + r
                    job_in(j + 1, (r + 1) % RING, t + (r + 1) // RING)
                    job_up(j, r, t, j - 2)
                    job_down(j - 2, (r - 2) % RING, expert_of(j - 2), t if r == 2 else t - 1)
            for j in range(JOBS - RING, JOBS + 2):
                if j + 1 < JOBS:
                    job_in(j + 1, (j + 1) % RING, (j + 1) // RING)
                if j < JOBS:
                    job_up(j, j % RING, j // RING, j - 2)
                job_down(j - 2, (j - 2) % RING, expert_of(j - 2), (j - 2) // RING)


def kernel(x, cond_8, L0_cond_W_base, L0_cond_b_base, L0_cond_As, L0_cond_Bs, L0_attn_Wq, L0_attn_Wk, L0_attn_Wv,
           L0_attn_Wg, L0_attn_Wo, L0_attn_gamma, L0_attn_beta, L0_cond2_W_up, L0_cond2_b_up, L0_cond2_W_gate,
           L0_cond2_b_gate, L0_cond2_W_down, L0_cond2_b_down, L0_ffn_router_w, L0_ffn_w1, L0_ffn_b1, L0_ffn_w2,
           L0_ffn_b2):
    import concourse.bacc as bacc
    from concourse.bass_utils import run_bass_kernel_spmd

    a = np.asarray
    at = np.arange(P)
    yrow = (at % 16) * E + 4 * (at % 32 // 16) + at // 32
    arrays = {
        "xT": a(x).transpose(2, 0, 1).reshape(P, NT),
        "w_first": np.concatenate([a(L0_cond_W_base).T, a(L0_cond_As).reshape(P, P).T], axis=1),
        "w_rest": np.concatenate([a(L0_cond_Bs).transpose(0, 2, 1).reshape(P, P), a(L0_attn_Wv).T, a(L0_attn_Wk).T,
                                  a(L0_attn_Wg).T, a(L0_attn_Wq).T, a(L0_attn_Wo).T[yrow]], axis=1),
        "w_upgate": np.concatenate([a(L0_cond2_W_up), a(L0_cond2_W_gate)], axis=1).transpose(2, 0, 1).reshape(P, -1),
        "w_down": a(L0_cond2_W_down).reshape(E, P, 2, P).transpose(3, 0, 2, 1).reshape(P, -1),
        "w_1": np.concatenate([a(L0_ffn_w1).transpose(0, 2, 1), a(L0_ffn_b1).reshape(E, FC, P).transpose(0, 2, 1)], axis=2),
        "w_2": a(L0_ffn_w2).reshape(E, P, FC, P).transpose(3, 0, 2, 1).reshape(P, -1),
        "cond_row": a(cond_8).reshape(1, -1),
        "cond_T": a(cond_8).T,
    }
    select = np.zeros((P, E, 32), np.float32)
    for e in range(E):
        select[at, e, 16 * (e // 4) + at // E] = 1
    ranks = np.tile(np.concatenate([E - np.arange(E), REGION * np.arange(E)]).astype(np.float32), (P, 1))
    columns = np.stack([a(L0_cond_b_base), a(L0_attn_gamma)[yrow], a(L0_attn_beta)[yrow]], axis=1)
    biases = np.concatenate([np.concatenate([a(L0_cond2_b_up), a(L0_cond2_b_gate)], axis=1).reshape(-1),
                             a(L0_cond2_b_down).reshape(-1),
                             a(L0_ffn_b2).reshape(-1)]).reshape(P, -1)
    arrays["small"] = np.concatenate([np.eye(P, dtype=np.float32), select.reshape(P, -1),
                                      np.triu(np.ones((P, P), np.float32), 1), ranks, a(L0_ffn_router_w).T,
                                      columns, biases], axis=1)
    row = np.arange(NB)
    arrays["dest"] = (GB * at[:, None, None] + (row // GB * GT + row % GB)[None, :, None]
                      + NT * np.arange(TOPK)[None, None, :]).astype(np.uint32).reshape(P, -1)
    arrays["job_no"] = np.stack([np.arange(JOBS), P * np.arange(JOBS)]).astype(np.float32).reshape(1, -1)

    nc = bacc.Bacc("TRN2", target_bir_lowering=False, num_devices=1)
    arrays = {k: np.ascontiguousarray(v) for k, v in arrays.items()}
    aps = {k: nc.dram_tensor(k, list(v.shape), mybir.dt.from_np(v.dtype), kind="ExternalInput").ap()
           for k, v in arrays.items()}
    out = nc.dram_tensor("out", [NB, P, P], F32, kind="ExternalOutput").ap()
    adaln_attn_ffn_kernel(nc, out=out, **aps)
    r = run_bass_kernel_spmd(nc, [arrays], core_ids=[0])
    return r.results[0]["out"]
```

```python
from contextlib import ExitStack

import numpy as np

import concourse.bass as bass
from concourse import mybir

F32 = mybir.dt.float32
BF16 = mybir.dt.bfloat16
I32 = mybir.dt.int32
U32 = mybir.dt.uint32
ALU = mybir.AluOpType
ACT = mybir.ActivationFunctionType
AX_X = mybir.AxisListType.X

P = 128
NB = 16
E = 8
NH = 16
GB = 4
NG = NB // GB
GT = GB * P
NT = NB * P
H2 = 256
FF = 512
FC = FF // P
TOPK = 2
LN_EPS = 1e-5
LORA_SCALE = 2.0
ROW = P + 2
REGION = NT + P
DUMMY = E * REGION
JOBS = (NT * TOPK + E * (P - 1)) // P
RING = 3
SPREAD = 3
NOWHERE = 1 << 20
BUG, BDO, B2O, NBIAS = 0, E * 2 * H2, E * (2 * H2 + P), E * (2 * H2 + 2 * P)
C_BEFORE = P + E * 32
C_RANKS = C_BEFORE + P
C_ROUTER = C_RANKS + 2 * E
C_COLS = C_ROUTER + E
C_B1 = C_COLS + 3
C_BIAS = C_B1 + E * FC
SMALL = C_BIAS + NBIAS // P
PIECES = [(g * GB, GB) for g in range(NG - 1)] + [(NB - GB, GB // 2), (NB - GB // 2, GB // 2)]
assert JOBS % (2 * RING) == RING


def adaln_attn_ffn_kernel(nc, xT, w_first, w_rest, w_spread, w_upgate, w_down, w_1, w_2, small, cond_row, cond_T,
                          dest, job_no, out):
    v_rows = nc.dram_tensor("v_rows", [NG, P, GT], F32).ap()
    bias_rows = nc.dram_tensor("bias_rows", [3, NBIAS], BF16).ap()
    routed = nc.dram_tensor("routed", [DUMMY + P, ROW], F32).ap()
    mixed = nc.dram_tensor("mixed", [TOPK * NT, P], F32).ap()

    with ExitStack() as ctx:
        def sb(name, shape, dt=F32):
            return ctx.enter_context(nc.sbuf_tensor(name, shape, dt))

        def sem(name):
            return ctx.enter_context(nc.semaphore(name))

        x_sb = sb("x_sb", [P, NT])
        wf = sb("wf", [P, 2 * P])
        wr = sb("wr", [P, 6 * P])
        wsp = sb("wsp", [P, SPREAD * P])
        wug = sb("wug", [P, E * 2 * H2])
        wd = sb("wd", [P, E * 2 * P])
        w1j = sb("w1j", [P, RING, FF])
        w2 = sb("w2", [P, E * FC * P])
        crow_w = sb("crow_w", [1, NB, E])
        ccol = sb("ccol", [P, NB])
        ccol2 = sb("ccol2", [P, NB])
        b_part = sb("b_part", [P, 3, NBIAS // P], BF16)
        b_rest = sb("b_rest", [P, 2, NBIAS // P])
        brow = sb("brow", [P, NBIAS], BF16)
        small_sb = sb("small_sb", [P, SMALL])
        ident = small_sb[:, 0:P]
        sel = small_sb[:, P:P + E * 32].rearrange("p (e c) -> p e c", e=E)
        bef_f = small_sb[:, C_BEFORE:C_BEFORE + P]
        rk = small_sb[:, C_RANKS:C_RANKS + 2 * E].rearrange("p (a e) -> p a e", a=2)
        wrt = small_sb[:, C_ROUTER:C_ROUTER + E]
        cols = small_sb[:, C_COLS:C_COLS + 3]
        b1 = small_sb[:, C_B1:C_B1 + E * FC]
        b_in = small_sb[:, C_BIAS:SMALL]
        bef = sb("bef", [P, P], BF16)
        ones = sb("ones", [P, P], BF16)
        dst = sb("dst", [P, NB, TOPK], U32)
        jno = sb("jno", [1, 2, JOBS])
        hs = sb("hs", [P, GT])
        xc = sb("xc", [P, GT])
        v_sb = sb("v_sb", [P, GT])
        k_sb = sb("k_sb", [P, NT])
        state = sb("state", [P, 2, E, GT])
        prod = sb("prod", [P, E, GT])
        y_sb = sb("y_sb", [P, GT])
        bst = sb("bst", [P, GB, 6])
        mv = sb("mv", [P, GB, 2])
        var = sb("var", [P, GB])
        sd = sb("sd", [P, GB])
        rstd = sb("rstd", [P, GB])
        z_sb = sb("z_sb", [P, GT])
        zn = sb("zn", [P, GT])
        x1T = sb("x1T", [P, GT])
        cmax = sb("cmax", [1, NB])
        ceq = sb("ceq", [1, NB, E])
        crk = sb("crk", [1, NB])
        cexp = sb("cexp", [1, NB], I32)
        silu_sb = sb("silu_sb", [P, GB, H2])
        hid = sb("hid", [P, GB, H2])
        hidT = sb("hidT", [P, GB, H2])
        c_sb = sb("c_sb", [P, GT])
        cT = sb("cT", [P, GT])
        rows = sb("rows", [P, 2, GB, TOPK, ROW])
        x1 = sb("x1", [P, NB, P])
        lg = sb("lg", [P, GB, E])
        lg2 = sb("lg2", [P, GB, E])
        m1 = sb("m1", [P, GB])
        m2 = sb("m2", [P, GB])
        eq = sb("eq", [P, GB, E])
        rr = sb("rr", [P, GB])
        oh1 = sb("oh1", [P, GB, E])
        oh2 = sb("oh2", [P, GB, E])
        rank = sb("rank", [P, GB, E])
        pick = sb("pick", [P, TOPK, GB, E])
        wdiff = sb("wdiff", [P, GB])
        gelu_warm = sb("gelu_warm", [P, 1])
        M = sb("M", [P, GB, E], BF16)
        msum = sb("msum", [P, E])
        Mpre = sb("Mpre", [P, E], BF16)
        slot_f = sb("slot_f", [P, TOPK, GB])
        slot = sb("slot", [P, 2, TOPK, GB], U32)
        cnt = sb("cnt", [1, E])
        ctiles = sb("ctiles", [1, E])
        cmp16 = sb("cmp16", [1, E, NB])
        cends = sb("cends", [1, E])
        ones_e = sb("ones_e", [1, E])
        jge = sb("jge", [1, JOBS, E])
        jex = sb("jex", [1, JOBS])
        jst = sb("jst", [1, JOBS])
        jok = sb("jok", [1, JOBS])
        jtmp = sb("jtmp", [1, JOBS])
        jrow = sb("jrow", [1, JOBS], I32)
        jwex = sb("jwex", [1, JOBS], I32)
        padf = sb("padf", [1, E])
        padr = sb("padr", [1, E], I32)
        pad = sb("pad", [P, ROW])
        late = state[:, :, :, :].rearrange("p g e t -> p (g e t)")
        at = [0]

        def carve(*shape):
            n = int(np.prod(shape))
            a = late[:, at[0]:at[0] + n]
            at[0] += n
            assert at[0] <= 2 * E * GT
            return a.rearrange({2: "p (a b) -> p a b", 3: "p (a b c) -> p a b c"}[len(shape)],
                               **dict(zip("abc", shape)))

        jin = carve(RING, ROW)
        jmeta = carve(JOBS, 2)
        jT = carve(RING, P)
        actT = carve(RING, FF)
        res = carve(RING, P)
        y0 = carve(NG, GT)
        y1 = carve(NG, GT)
        jidx = sb("jidx", [P, RING], U32)

        bank = [ctx.enter_context(nc.psum_tensor(f"bank{i}", [P, GT], F32)) for i in range(8)]
        B_XC, B_HK, B_A, B_Q, B_Y = bank[0:5]
        spread_bank = bank[4:4 + SPREAD]
        B_ROW, B_W = bank[5:7], bank[7]
        J_H, J_X, J_O = bank[0:3], bank[3], bank[4:7]

        names = """s_x0 s_x s_wf s_wr s_wsp s_cond s_small s_crow s_late s_ugd s_w2 s_bias_out s_bias_rows s_pad s_padrow s_vst s_out
            ones_ready brow_zero before_ready bias_split expert_ready ccol_ready
            pe_h pe_xc pe_v pe_k pe_g pe_q pe_spread pe_y pe_yt pe_zt pe_o
            act_hs act_xc act_v act_k act_a act_y act_sd act_zn
            kv_ready own_kv a_zeroed scanned prod_ready dve_chain norm_chain route_chain stats_ready var_ready z_ready x1_ready
            pe_ug pe_ht pe_c pe_ct pe_l pe_x1 pe_rank
            silu_done hid_ready hidT_ready c_ready cT_ready x1_copied
            lg_copied wdiff_ready chosen placed rows_free slot_ready rows_ready jobs_ready
            pads_ready pe_jx pe_jh pe_jo jT_ready jin_free gelu_done added""".split()
        S = {n: sem(n) for n in names}
        s_vload = [sem(f"s_vload{e}") for e in range(E)]
        s_job = [sem(f"s_job{r}") for r in range(RING)]
        s_put_idx = [sem(f"s_put_idx{r}") for r in range(RING)]
        s_put_res = [sem(f"s_put_res{r}") for r in range(RING)]
        s_put = [sem(f"s_put{r}") for r in range(RING)]
        s_scatter = [sem(f"s_scatter{b}") for b in range(2)]
        s_w1j = [sem(f"s_w1j{r}") for r in range(RING)]
        s_y = [sem(f"s_y{i}") for i in range(len(PIECES))]

        block = ctx.enter_context(nc.Block())

        def grp(g):
            return bass.ds(g * GT, GT)

        def row_place(n, last):
            return ((B_ROW + [B_A, B_Q])[n], n) if last else (B_ROW[n % 2], n % 2)

        def side(g):
            return (NG - 1 - g) % 2 if isinstance(g, int) and g >= NG - 3 else 1

        def rows_sent_before(eng, g):
            if not isinstance(g, int):
                eng.wait_ge(S["rows_free"], g + 1)
            elif g >= NG - 2:
                eng.wait_ge(S["rows_free"], g)

        def pad_experts(eng, half):
            eng.wait_ge(S["pads_ready"], 1)
            with eng.Fori(half * (E // 2), (half + 1) * (E // 2)) as e:
                r = eng.value_load(padr[0:1, bass.ds(e, 1)], min_val=0, max_val=DUMMY - P)
                eng.dma_start(routed[bass.ds(r, P), :], pad[:, :]).then_inc(S["s_padrow"], 16)

        def load_weights(eng, j, r, used):
            e = eng.value_load(jwex[0:1, bass.ds(j, 1)], min_val=0, max_val=E - 1)
            if used is not None:
                eng.wait_ge(S["pe_jh"], used)
            eng.dma_start(w1j[:, r, :], w_1[bass.ds(e, 1), :, :].rearrange("e p f -> p (e f)")).then_inc(s_w1j[r], 16)

        def load_results(eng, k, y):
            for r in range(RING):
                eng.wait_ge(s_put[r], 16 * (JOBS // RING))
            for i, (b, n) in enumerate(PIECES):
                g, cols = b // GB, slice(b % GB * P, (b % GB + n) * P)
                src = mixed[k * NT + g * GT:k * NT + (g + 1) * GT, :].rearrange("(p b) d -> p (b d)", p=P)
                eng.dma_start(y[:, g, cols], src[:, cols]).then_inc(s_y[i], 16)

        @block.sync
        def _(sp):
            sp.dma_start(wf[:, :], w_first).then_inc(S["s_wf"], 16)
            sp.dma_start(x_sb[:, 0:GT], xT[:, 0:GT]).then_inc(S["s_x0"], 16)
            sp.dma_start(wr[:, :], w_rest).then_inc(S["s_wr"], 16)
            sp.dma_start(wsp[:, :], w_spread).then_inc(S["s_wsp"], 16)
            sp.dma_start(x_sb[:, GT:NT], xT[:, GT:NT]).then_inc(S["s_x"], 16)

            def spread_v(g, used):
                sp.wait_ge(S["act_v"], g + 1)
                sp.dma_start(v_rows[bass.ds(g, 1), :, :].rearrange("g p t -> p (g t)"), v_sb[:, :]).then_inc(S["s_vst"], 16)
                sp.wait_ge(S["s_vst"], g * 16 + 16)
                for e in range(SPREAD if isinstance(g, int) and g == 0 else 0, E):
                    if used is not None:
                        sp.wait_ge(S["prod_ready"], used * E + e + 1)
                    src = v_rows[bass.ds(g, 1), :, :].rearrange("g (h e) t -> (g h) e t", e=E)[:, e, :]
                    sp.dma_start(state[:, bass.ds(g % 2, 1), e, :].rearrange("p g t -> p (g t)"),
                                 src.unsqueeze(1).broadcast_to([NH, E, GT])).then_inc(s_vload[e], 16)

            spread_v(0, None)
            spread_v(1, None)
            sp.dma_start(wug[:, :], w_upgate).then_inc(S["s_ugd"], 16)
            sp.dma_start(wd[:, :], w_down).then_inc(S["s_ugd"], 16)
            sp.dma_start(w2[:, :], w_2).then_inc(S["s_w2"], 16)

            def rows_sent(b, n):
                sp.wait_ge(s_scatter[b], n * (16 * GB * TOPK))
                sp.sem_inc(S["rows_free"], 1)

            spread_v(2, 0)
            with sp.Fori(1, NG - 2) as g:
                spread_v(g + 2, g)
                rows_sent(1, g)
            rows_sent(0, 1)
            sp.wait_ge(S["s_pad"], 3)
            sp.dma_start(routed[DUMMY:DUMMY + P, :], pad[:, :]).then_inc(S["s_padrow"], 16)
            pad_experts(sp, 0)

            sp.wait_ge(S["jobs_ready"], 1)
            for r in range(RING):
                load_weights(sp, r, r, None)
            sp.wait_ge(S["s_padrow"], 16 * (E + 1))
            sp.wait_ge(s_scatter[0], 2 * (16 * GB * TOPK))
            sp.wait_ge(s_scatter[1], (NG - 2) * (16 * GB * TOPK))
            for r in range(RING):
                row = sp.value_load(jrow[0:1, r:r + 1], min_val=0, max_val=DUMMY)
                sp.dma_start(jin[:, r, :], routed[bass.ds(row, P), :]).then_inc(s_job[r], 16)
            with sp.Fori(0, JOBS // (2 * RING)) as u:
                for i in range(2 * RING):
                    j, r = u * (2 * RING) + RING + i, i % RING
                    row = sp.value_load(jrow[0:1, bass.ds(j, 1)], min_val=0, max_val=DUMMY)
                    sp.wait_ge(S["jin_free"], j - 2)
                    sp.dma_start(jin[:, r, :], routed[bass.ds(row, P), :]).then_inc(s_job[r], 16)
                    if (RING + i) % 2 == 1:
                        load_weights(sp, j, r, j - 2)
            load_results(sp, 0, y0)
            for i, (b, n) in enumerate(PIECES):
                sp.wait_ge(S["added"], i + 1)
                sp.dma_start(out[b:b + n].rearrange("b p d -> p b d"),
                             y0[:, b // GB, b % GB * P:(b % GB + n) * P].rearrange("p (b d) -> p b d", d=P)).then_inc(S["s_out"], 16)
            sp.wait_ge(S["s_out"], 16 * len(PIECES))

        @block.gpsimd
        def _(pool):
            pool.memset(ones[:, :], 1.0).then_inc(S["ones_ready"], 1)
            pool.memset(pad[:, 0:P], 0.0).then_inc(S["s_pad"], 1)
            pool.memset(pad[:, P:P + 1].bitcast(U32), NOWHERE).then_inc(S["s_pad"], 1)
            pool.memset(pad[:, P + 1:ROW], 0.0).then_inc(S["s_pad"], 1)
            pool.memset(brow[:, :].bitcast(U32), 0).then_inc(S["brow_zero"], 1)
            pool.wait_ge(S["bias_split"], 3)
            pool.dma_start(bias_rows.rearrange("k (p n) -> p k n", p=P), b_part[:, :, :]).then_inc(S["s_bias_out"], 16)

            def key_value(g):
                half = g % 2 if isinstance(g, int) else pool.snap(g % 2)
                pool.wait_ge(S["act_k"], g + 1)
                first = isinstance(g, int) and g == 0
                for e in range(SPREAD if first else 0, E):
                    pool.wait_ge(s_vload[e], g * 16 if e < SPREAD else g * 16 + 16)
                    st = state[:, bass.ds(half, 1), e, :].rearrange("p g t -> p (g t)")
                    pool.tensor_tensor(st, st, k_sb[:, grp(g)], ALU.mult).then_inc(S["kv_ready"], 1)

            def scatter(groups, b):
                pool.wait_ge(S["brow_zero"], 1)
                pool.wait_ge(S["slot_ready"], groups)
                pool.wait_ge(S["rows_ready"], groups)
                for i in range(GB):
                    for k in range(TOPK):
                        pool.indirect_dma_start(
                            out=routed, out_offset=bass.IndirectOffsetOnAxis(ap=slot[:, b, k, i:i + 1], axis=0),
                            in_=rows[:, b, i, k, :], in_offset=None,
                            bounds_check=DUMMY - 1, oob_is_err=False).then_inc(s_scatter[b], 16)

            pool.wait_ge(S["s_bias_out"], 16)
            pool.wait_ge(S["brow_zero"], 1)
            pool.dma_start(brow[0:3, :], bias_rows).then_inc(S["s_bias_rows"], 16)
            for g in range(3):
                key_value(g)
            with pool.Fori(1, NG - 2) as g:
                key_value(g + 2)
                scatter(g, 1)
            for n in range(NG - 2, NG + 1):
                scatter(n, side(n - 1))
            with pool.Fori(1, JOBS // RING + 1) as n:
                for r in range(RING):
                    pool.wait_ge(S["brow_zero"], 1)
                    pool.wait_ge(s_put_idx[r], n)
                    pool.wait_ge(s_put_res[r], n)
                    pool.indirect_dma_start(
                        out=mixed, out_offset=bass.IndirectOffsetOnAxis(ap=jidx[:, r:r + 1], axis=0),
                        in_=res[:, r, :], in_offset=None,
                        bounds_check=TOPK * NT - 1, oob_is_err=False).then_inc(s_put[r], 16)

        @block.scalar
        def _(act):
            act.dma_start(ccol[:, :], cond_T.unsqueeze(1).broadcast_to([E, NH, NB])).then_inc(S["s_cond"], 16)
            act.dma_start(small_sb[:, :], small).then_inc(S["s_small"], 16)
            act.dma_start(crow_w[:, :, :].rearrange("p b e -> p (b e)"), cond_row).then_inc(S["s_crow"], 16)
            act.dma_start(dst[:, :, :].rearrange("p b k -> p (b k)"), dest).then_inc(S["s_late"], 16)
            act.dma_start(jno[:, :, :].rearrange("p j e -> p (j e)"), job_no).then_inc(S["s_late"], 16)
            act.wait_ge(S["s_cond"], 16)
            act.activation(ccol2[:, :], ccol[:, :], ACT.Copy, scale=LORA_SCALE).then_inc(S["ccol_ready"], 1)
            act.wait_ge(S["ccol_ready"], 1)
            act.wait_ge(S["s_small"], 16)

            def take_h(g):
                act.wait_ge(S["pe_h"], g + 1)
                for i in range(GB):
                    last = act.activation(hs[:, i * P:(i + 1) * P], B_HK[:, i * P:(i + 1) * P], ACT.Copy,
                                          scale=ccol2[:, bass.ds(g * GB + i, 1)])
                last.then_inc(S["act_hs"], 1)

            def take_xc(g):
                act.wait_ge(S["pe_xc"], g + 1)
                act.wait_ge(S["pe_q"], g)
                act.activation(xc[:, :], B_XC[:, :], ACT.Identity, bias=cols[:, 0:1]).then_inc(S["act_xc"], 1)

            def take_v(g):
                act.wait_ge(S["pe_v"], g + 1)
                act.wait_ge(S["s_vst"], g * 16)
                act.activation(v_sb[:, :], B_XC[:, :], ACT.Copy).then_inc(S["act_v"], 1)

            def take_k(g):
                act.wait_ge(S["pe_k"], g + 1)
                act.activation(k_sb[:, grp(g)], B_HK[:, :], ACT.Copy).then_inc(S["act_k"], 1)

            def gate(g):
                act.wait_ge(S["pe_g"], g + 1)
                act.activation(B_A[:, :], B_A[:, :], ACT.Sigmoid).then_inc(S["act_a"], 1)

            def take_y(g):
                act.wait_ge(S["pe_y"], g + 1)
                act.activation(y_sb[:, :], B_Y[:, :], ACT.Copy).then_inc(S["act_y"], 1)

            def root(g):
                act.wait_ge(S["var_ready"], g + 1)
                act.activation(sd[:, :], var[:, :], ACT.Sqrt).then_inc(S["act_sd"], 1)

            def take_z(g):
                act.wait_ge(S["pe_zt"], g + 1)
                act.activation(zn[:, :], B_Y[:, :], ACT.Identity, bias=cols[:, 2:3], scale=cols[:, 1:2]).then_inc(S["act_zn"], 1)

            def silu(g, n, last=False):
                bank, r = row_place(n, last)
                act.wait_ge(S["pe_ug"], g * GB + n + 1)
                act.activation(silu_sb[:, r, :], bank[:, 0:H2], ACT.Silu).then_inc(S["silu_done"], 1)

            def take_hidT(g, n, last=False):
                bank, r = row_place(n, last)
                act.wait_ge(S["pe_ht"], g * GB + n + 1)
                act.activation(hidT[:, r, :], bank[:, 0:H2], ACT.Copy).then_inc(S["hidT_ready"], 1)

            def take_c(g, n, last=False):
                bank, r = row_place(n, last)
                act.wait_ge(S["pe_c"], g * GB + n + 1)
                act.activation(c_sb[:, n * P:(n + 1) * P], bank[:, 0:P], ACT.Copy).then_inc(S["c_ready"], 1)

            def take_cT(g):
                act.wait_ge(S["pe_ct"], g + 1)
                act.activation(cT[:, :], B_W[:, :], ACT.Copy).then_inc(S["cT_ready"], 1)

            def take_x1(g):
                act.wait_ge(S["pe_x1"], g + 1)
                act.activation(x1[:, bass.ds(g * GB, GB), :].rearrange("p b d -> p (b d)"),
                               B_Y[:, :], ACT.Copy).then_inc(S["x1_copied"], 1)

            def row_values(g):
                act.wait_ge(S["c_ready"], g * GB + GB)
                rows_sent_before(act, g)
                for k in range(TOPK):
                    act.activation(rows[:, side(g), :, k, 0:P], c_sb[:, :].rearrange("p (b d) -> p b d", d=P), ACT.Copy)

            def row_weights(g):
                act.wait_ge(S["wdiff_ready"], g + 1)
                for k in range(TOPK):
                    last = act.activation(rows[:, side(g), :, k, P + 1:ROW].rearrange("p b o -> p (b o)"), wdiff[:, :],
                                          ACT.Sigmoid, scale=1.0 if k == 1 else -1.0)
                last.then_inc(S["rows_ready"], 1)

            def step(g, first, ahead):
                gate(g + 1)
                take_y(g)
                if not first:
                    for n in range(2, GB):
                        silu(g - 1, n)
                root(g)
                if not first:
                    for n in range(2, GB):
                        take_hidT(g - 1, n)
                if ahead:
                    take_h(g + 2)
                if not first:
                    for n in range(2, GB):
                        take_c(g - 1, n)
                take_z(g)
                if ahead:
                    take_xc(g + 2)
                if not first:
                    take_cT(g - 1)
                if ahead:
                    take_v(g + 2)
                if not first:
                    row_values(g - 1)
                silu(g, 0)
                silu(g, 1)
                take_x1(g)
                if ahead:
                    take_k(g + 2)
                for n in range(2):
                    take_hidT(g, n)
                for n in range(2):
                    take_c(g, n)
                if not ahead:
                    for n in range(2, GB):
                        silu(g, n)
                elif not first:
                    row_weights(g - 1)

            act.sem_inc(S["rows_free"], 1)
            take_h(0)
            take_xc(0)
            take_v(0)
            take_k(0)
            gate(0)
            take_h(1)
            take_xc(1)
            take_v(1)
            take_k(1)
            step(0, True, True)
            with act.Fori(1, NG - 2) as g:
                step(g, False, True)
            step(NG - 2, False, False)
            g = NG - 1
            take_y(g)
            row_weights(g - 2)
            for n in range(2, GB):
                take_hidT(g - 1, n)
            root(g)
            for n in range(2, GB):
                take_c(g - 1, n)
            take_cT(g - 1)
            take_z(g)
            row_values(g - 1)
            for n in range(GB):
                silu(g, n, True)
                if n >= 2:
                    take_hidT(g, n - 2, True)
            row_weights(g - 1)
            for n in range(2, GB):
                take_hidT(g, n, True)
                take_c(g, n - 2, True)
            for n in range(2, GB):
                take_c(g, n, True)
            take_cT(g)
            row_values(g)
            row_weights(g)
            take_x1(g)
            act.activation(gelu_warm[:, :], wdiff[:, 0:1], ACT.Gelu)
            act.wait_ge(S["s_pad"], 3)
            pad_experts(act, 1)

            def gelu(j, r, used):
                e = act.value_load(jwex[0:1, bass.ds(j, 1)], min_val=0, max_val=E - 1)
                act.wait_ge(S["pe_jh"], j + 1)
                if used is not None:
                    act.wait_ge(S["pe_jo"], used)
                for c in range(FC):
                    last = act.activation(actT[:, r, c * P:(c + 1) * P], J_H[r][:, c * P:(c + 1) * P], ACT.Gelu,
                                          bias=b1[:, bass.ds(e * FC + c, 1)])
                last.then_inc(S["gelu_done"], 1)

            act.wait_ge(S["jobs_ready"], 1)
            def next_weights(j, i):
                load_weights(act, j + RING, i % RING, None)

            for j in range(RING):
                gelu(j, j, None)
                if (j + RING) % 2 == 0:
                    next_weights(j, j)
            with act.Fori(0, JOBS // (2 * RING) - 1) as u:
                for i in range(2 * RING):
                    j = u * (2 * RING) + RING + i
                    gelu(j, i % RING, j - 2)
                    if i % 2 == 0:
                        next_weights(j, i)
            for j in range(JOBS - 2 * RING, JOBS):
                gelu(j, j % RING, j - 2)
                if j + RING < JOBS and (j + RING) % 2 == 0:
                    next_weights(j, j)
            load_results(act, 1, y1)

        @block.vector
        def _(dve):
            def chain(name, base):
                done = [base]

                def link(ins, between=None, k=None):
                    done[0] = done[0] + 1
                    ins.then_inc(S[name], 1)
                    if between is not None:
                        between(k)
                    dve.wait_ge(S[name], done[0])
                return link

            link = chain("dve_chain", 0)
            dve.wait_ge(S["s_small"], 16)
            dve.wait_ge(S["s_crow"], 16)
            link(dve.reduce_max(cmax[:, :], crow_w[:, :, :], AX_X))
            link(dve.tensor_tensor(ceq[:, :, :], crow_w[:, :, :], cmax[:, :].unsqueeze(2).broadcast_to([1, NB, E]), ALU.is_equal))
            link(dve.tensor_tensor(ceq[:, :, :], ceq[:, :, :], rk[0:1, 0:1, :].broadcast_to([1, NB, E]), ALU.mult))
            link(dve.reduce_max(crk[:, :], ceq[:, :, :], AX_X))
            dve.tensor_scalar(cexp[:, :], crk[:, :], -1.0, float(E), ALU.mult, ALU.add).then_inc(S["expert_ready"], 1)
            dve.tensor_copy(b_part[:, 0, :], b_in[:, :]).then_inc(S["bias_split"], 1)
            dve.wait_ge(S["bias_split"], 1)
            link(dve.tensor_tensor(b_rest[:, 0, :], b_in[:, :], b_part[:, 0, :], ALU.subtract))
            dve.tensor_copy(b_part[:, 1, :], b_rest[:, 0, :]).then_inc(S["bias_split"], 1)
            dve.wait_ge(S["bias_split"], 2)
            link(dve.tensor_tensor(b_rest[:, 1, :], b_rest[:, 0, :], b_part[:, 1, :], ALU.subtract))
            dve.tensor_copy(b_part[:, 2, :], b_rest[:, 1, :]).then_inc(S["bias_split"], 1)
            dve.tensor_copy(bef[:, :], bef_f[:, :]).then_inc(S["before_ready"], 1)
            link(dve.memset(ones_e[:, :], 1.0))
            link(dve.memset(Mpre[:, :], 0.0))
            def unit(g, product, e):
                st = state[:, bass.ds(g % 2, 1), e, :].rearrange("p g t -> p (g t)")
                if not product:
                    if isinstance(g, int) and g == 0 and e < SPREAD:
                        dve.wait_ge(S["own_kv"], e + 1)
                    else:
                        dve.wait_ge(S["kv_ready"], g * E + e + 1 - SPREAD)
                    dve.tensor_tensor_scan(st, B_A[:, :], st, 0.0, ALU.mult, ALU.add).then_inc(S["scanned"], 1)
                else:
                    dve.wait_ge(S["scanned"], g * E + e + 1)
                    if e == 0:
                        dve.wait_ge(S["pe_y"], g)
                    dve.tensor_tensor(prod[:, e, :], st, B_Q[:, :], ALU.mult).then_inc(S["prod_ready"], 1)

            def cut_states(g):
                dve.wait_ge(S["act_a"], g + 1)
                dve.memset(B_A[:, :].rearrange("p (b t) -> p b t", t=P)[:, :, 0:1], 0.0).then_inc(S["a_zeroed"], 1)
                dve.wait_ge(S["a_zeroed"], g + 1)

            def start_states(g):
                cut_states(g)
                unit(g, False, 0)
                dve.wait_ge(S["pe_q"], g + 1)

            def units(g, lo, hi):
                for e in range(lo, hi):
                    if e < E:
                        unit(g, False, e)
                    unit(g, True, e - 1)

            NORM_LINKS, ROUTE_LINKS = 2, 14

            def norm_stats(g, link):
                dve.wait_ge(S["pe_yt"], g + 1)
                for i in range(GB):
                    last = dve.bn_stats(bst[:, i, :], B_Y[:, i * P:(i + 1) * P])
                last.then_inc(S["stats_ready"], 1)
                n_stats = g + 1 if isinstance(g, int) else dve.snap(g + 1)
                dve.wait_ge(S["s_small"], 16)
                dve.wait_ge(S["stats_ready"], n_stats)
                for i in range(GB):
                    last = dve.bn_aggr(mv[:, i, :], bst[:, i, :])
                link(last)
                dve.tensor_scalar(var[:, :], mv[:, :, 1], LN_EPS, None, ALU.add).then_inc(S["var_ready"], 1)

            def norm_apply(g, link):
                dve.wait_ge(S["act_sd"], g + 1)
                link(dve.reciprocal(rstd[:, :], sd[:, :]))
                for i in range(GB):
                    last = dve.tensor_scalar(z_sb[:, i * P:(i + 1) * P], B_Y[:, i * P:(i + 1) * P],
                                             mv[:, i, 0:1], rstd[:, i:i + 1], ALU.subtract, ALU.mult)
                last.then_inc(S["z_ready"], 1)

            def residual(g):
                dve.wait_ge(S["pe_o"], g + 1)
                dve.tensor_tensor(x1T[:, :], x_sb[:, grp(g)], B_Y[:, :], ALU.add).then_inc(S["x1_ready"], 1)

            def hidden(g, n, last=False):
                bank, r = row_place(n, last)
                dve.wait_ge(S["silu_done"], g * GB + n + 1)
                dve.tensor_tensor(hid[:, r, :], silu_sb[:, r, :], bank[:, H2:2 * H2],
                                  ALU.mult).then_inc(S["hid_ready"], 1)

            def spread(ap):
                return ap.unsqueeze(2).broadcast_to([P, GB, E])

            def route(g, link, between=None):
                dve.wait_ge(S["pe_l"], g + 1)
                dve.tensor_copy(lg[:, :, :].rearrange("p b e -> p (b e)"), B_W[:, 0:GB * E]).then_inc(S["lg_copied"], 1)
                dve.wait_ge(S["lg_copied"], g + 1)
                for k, (scores, most, onehot) in enumerate(((lg, m1, oh1), (lg2, m2, oh2))):
                    link(dve.reduce_max(most[:, :], scores[:, :, :], AX_X), between, 6 * k)
                    if k == 1:
                        dve.tensor_tensor(wdiff[:, :], m2[:, :], m1[:, :], ALU.subtract).then_inc(S["wdiff_ready"], 1)
                    link(dve.tensor_tensor(eq[:, :, :], scores[:, :, :], spread(most[:, :]), ALU.is_equal), between, 6 * k + 1)
                    link(dve.tensor_tensor(eq[:, :, :], eq[:, :, :], rk[:, 0:1, :].broadcast_to([P, GB, E]), ALU.mult), between, 6 * k + 2)
                    link(dve.reduce_max(rr[:, :], eq[:, :, :], AX_X), between, 6 * k + 3)
                    link(dve.tensor_tensor(onehot[:, :, :], rk[:, 0:1, :].broadcast_to([P, GB, E]), spread(rr[:, :]), ALU.is_equal), between, 6 * k + 4)
                    if scores is lg:
                        link(dve.scalar_tensor_tensor(lg2[:, :, :].rearrange("p b e -> p (b e)"),
                                                      oh1[:, :, :].rearrange("p b e -> p (b e)"), -3.0e38,
                                                      lg[:, :, :].rearrange("p b e -> p (b e)"), ALU.mult, ALU.add), between, 5)

            def choose(g, link):
                dve.tensor_tensor(M[:, :, :], oh1[:, :, :], oh2[:, :, :], ALU.add).then_inc(S["chosen"], 1)

            def place(g, link):
                dve.wait_ge(S["pe_rank"], g + 1)
                dve.tensor_tensor(rank[:, :, :], B_W[:, 0:GB * E].rearrange("p (b e) -> p b e", e=E),
                                  rk[:, 1:2, :].broadcast_to([P, GB, E]), ALU.add).then_inc(S["placed"], 1)
                link(dve.reduce_sum(msum[:, :], M[:, :, :].rearrange("p b e -> p e b"), AX_X))
                dve.tensor_tensor(Mpre[:, :], Mpre[:, :], msum[:, :], ALU.add)
                dve.wait_ge(S["placed"], g + 1)
                dve.tensor_tensor(pick[:, 0, :, :], rank[:, :, :], oh1[:, :, :], ALU.mult)
                link(dve.tensor_tensor(pick[:, 1, :, :], rank[:, :, :], oh2[:, :, :], ALU.mult))
                link(dve.reduce_sum(slot_f[:, :, :], pick[:, :, :, :], AX_X))
                rows_sent_before(dve, g)
                dve.tensor_copy(rows[:, side(g), :, :, P:P + 1].bitcast(U32).rearrange("p b k o -> p b (k o)"),
                                dst[:, bass.ds(g * GB, GB), :])
                dve.tensor_copy(slot[:, side(g), :, :], slot_f[:, :, :]).then_inc(S["slot_ready"], 1)

            def step(g, first):
                norm_link = chain("norm_chain", g * NORM_LINKS)
                route_link = chain("route_chain", (g - 1) * ROUTE_LINKS)
                start_states(g + 1)
                units(g + 1, 1, 3)
                norm_stats(g, norm_link)
                if not first:
                    hidden(g - 1, 2)
                    hidden(g - 1, 3)
                units(g + 1, 3, 4)
                norm_apply(g, norm_link)
                units(g + 1, 4, 5)
                residual(g)
                units(g + 1, 5, 6)

                def during_route(k):
                    if k == 1:
                        unit(g + 1, False, 6)
                    if k == 3:
                        unit(g + 1, True, 5)
                    if k == 5:
                        hidden(g, 0)
                    if k == 6:
                        hidden(g, 1)
                    if k == 8:
                        unit(g + 1, False, 7)
                    if k == 9:
                        unit(g + 1, True, 6)
                    if k == 10:
                        unit(g + 1, True, 7)

                if first:
                    hidden(g, 0)
                    hidden(g, 1)
                    units(g + 1, 6, E + 1)
                else:
                    route(g - 1, route_link, during_route)
                    choose(g - 1, route_link)
                if not first:
                    place(g - 1, route_link)

            dve.wait_ge(S["act_k"], 1)
            for e in range(SPREAD):
                dve.wait_ge(S["pe_spread"], e + 1)
                dve.tensor_tensor(state[:, 0, e, :], spread_bank[e][:, :], k_sb[:, 0:GT], ALU.mult).then_inc(S["own_kv"], 1)
                if e == 0:
                    cut_states(0)
                unit(0, False, e)
            dve.wait_ge(S["pe_q"], 1)
            for e in range(SPREAD - 1):
                unit(0, True, e)
            units(0, SPREAD, E + 1)
            dve.wait_ge(S["s_late"], 32)
            step(0, True)
            with dve.Fori(1, NG - 2) as g:
                step(g, False)
            step(NG - 2, False)
            g = NG - 1
            norm_link = chain("norm_chain", g * NORM_LINKS)
            route_link = chain("route_chain", (g - 1) * ROUTE_LINKS)
            hidden(g - 1, 2)
            hidden(g - 1, 3)
            norm_stats(g, norm_link)
            norm_apply(g, norm_link)
            residual(g)

            def hidden_during_route(k):
                if k in (4, 9):
                    hidden(g, (k - 4) // 5, True)

            route(g - 1, route_link, hidden_during_route)
            choose(g - 1, route_link)
            hidden(g, 2, True)
            place(g - 1, route_link)
            hidden(g, 3, True)
            route_link = chain("route_chain", g * ROUTE_LINKS)
            route(g, route_link)
            choose(g, route_link)
            place(g, route_link)

            link(dve.tensor_copy(cnt[:, :], B_W[0:1, GB * E:(GB + 1) * E]))
            link(dve.tensor_tensor(padf[:, :], cnt[:, :], rk[0:1, 1, :], ALU.add))
            dve.tensor_copy(padr[:, :], padf[:, :]).then_inc(S["pads_ready"], 1)
            link(dve.tensor_tensor(cmp16[:, :, :], cnt[:, :].unsqueeze(2).broadcast_to([1, E, NB]),
                                   jno[0:1, 1:2, 0:NB].broadcast_to([1, E, NB]), ALU.is_gt))
            link(dve.reduce_sum(ctiles[:, :], cmp16[:, :, :], AX_X))
            link(dve.tensor_tensor_scan(cends[:, :], ones_e[:, :], ctiles[:, :], 0.0, ALU.mult, ALU.add))
            jn = jno[:, 0, :]
            link(dve.tensor_tensor(jge[:, :, :], cends[:, :].unsqueeze(1).broadcast_to([1, JOBS, E]),
                                   jn.unsqueeze(2).broadcast_to([1, JOBS, E]), ALU.is_le))
            link(dve.reduce_sum(jex[:, :], jge[:, :, :], AX_X))
            link(dve.tensor_tensor(jge[:, :, :], jge[:, :, :], ctiles[:, :].unsqueeze(1).broadcast_to([1, JOBS, E]), ALU.mult))
            link(dve.reduce_sum(jst[:, :], jge[:, :, :], AX_X))
            link(dve.tensor_tensor(jst[:, :], jn, jst[:, :], ALU.subtract))
            link(dve.tensor_scalar(jok[:, :], jex[:, :], E - 0.5, float(P), ALU.is_lt, ALU.mult))
            link(dve.tensor_tensor(jst[:, :], jst[:, :], jok[:, :], ALU.mult))
            link(dve.tensor_scalar(jtmp[:, :], jex[:, :], float(REGION), None, ALU.mult))
            link(dve.tensor_tensor(jrow[:, :], jst[:, :], jtmp[:, :], ALU.add))
            dve.tensor_scalar(jwex[:, :], jex[:, :], float(E - 1), None, ALU.min).then_inc(S["jobs_ready"], 1)

            def job_in(j, r):
                dve.wait_ge(S["pe_jx"], j + 1)
                dve.tensor_copy(jT[:, r, :], J_X[:, 0:P]).then_inc(S["jT_ready"], 1)
                meta = jmeta[:, bass.ds(j, 1), :].rearrange("p j c -> p (j c)")
                dve.tensor_copy(meta[:, 0:1].bitcast(U32), jin[:, r, P:P + 1].bitcast(U32))
                dve.tensor_copy(meta[:, 1:2], jin[:, r, P + 1:ROW]).then_inc(S["jin_free"], 1)

            def job_out(j, r, t):
                dve.wait_ge(S["pe_jo"], j + 1)
                if not (isinstance(t, int) and t == 0):
                    dve.wait_ge(s_put[r], t * 16)
                dve.wait_ge(S["jin_free"], j + 1)
                meta = jmeta[:, bass.ds(j, 1), :].rearrange("p j c -> p (j c)")
                dve.tensor_copy(jidx[:, r:r + 1], meta[:, 0:1].bitcast(U32)).then_inc(s_put_idx[r], 1)
                dve.tensor_scalar(res[:, r, :], J_O[r][:, 0:P], meta[:, 1:2], None, ALU.mult).then_inc(s_put_res[r], 1)

            job_in(0, 0)
            for j in range(2 * RING):
                job_in(j + 1, (j + 1) % RING)
                if j >= 2:
                    job_out(j - 2, (j - 2) % RING, (j - 2) // RING)
            with dve.Fori(2, JOBS // RING - 1) as t:
                for r in range(RING):
                    job_in(t * RING + r + 1, (r + 1) % RING)
                    job_out(t * RING + r - 2, (r - 2) % RING, t if r == 2 else t - 1)
            for j in range(JOBS - RING, JOBS + 2):
                if j + 1 < JOBS:
                    job_in(j + 1, (j + 1) % RING)
                job_out(j - 2, (j - 2) % RING, (j - 2) // RING)

            for i, (b, n) in enumerate(PIECES):
                dve.wait_ge(s_y[i], 32)
                g, cols = b // GB, slice(b % GB * P, (b % GB + n) * P)
                link(dve.tensor_tensor(y0[:, g, cols], y0[:, g, cols], y1[:, g, cols], ALU.add))
                dve.tensor_tensor(y0[:, g, cols], y0[:, g, cols], x1[:, b:b + n, :].rearrange("p b d -> p (b d)"),
                                  ALU.add).then_inc(S["added"], 1)

        @block.tensor
        def _(pe):
            def w(k):
                return wr[:, k * P:(k + 1) * P]

            def project_h(g):
                pe.wait_ge(S["act_k"], g)
                pe.wait_ge(S["act_v"], g)
                pe.matmul(B_HK[:, :], wf[:, P:2 * P], x_sb[:, grp(g)], start=True, stop=True).then_inc(S["pe_h"], 1)
                pe.matmul(B_XC[:, :], wf[:, 0:P], x_sb[:, grp(g)], start=True, stop=False)

            def project_c(g):
                pe.wait_ge(S["act_hs"], g + 1)
                pe.matmul(B_XC[:, :], w(0), hs[:, :], start=False, stop=True).then_inc(S["pe_xc"], 1)

            def project_vk(g, which):
                if which == 0:
                    pe.wait_ge(S["act_xc"], g + 1)
                    pe.matmul(B_XC[:, :], w(1), xc[:, :], start=True, stop=True).then_inc(S["pe_v"], 1)
                else:
                    pe.matmul(B_HK[:, :], w(2), xc[:, :], start=True, stop=True).then_inc(S["pe_k"], 1)

            def gate_q(g, which):
                if which == 0:
                    pe.wait_ge(S["prod_ready"], g * E)
                    pe.matmul(B_A[:, :], w(3), xc[:, :], start=True, stop=True).then_inc(S["pe_g"], 1)
                else:
                    pe.matmul(B_Q[:, :], w(4), xc[:, :], start=True, stop=True).then_inc(S["pe_q"], 1)

            def reduce_y(g, r, first):
                if r == 0 and not first:
                    pe.wait_ge(S["x1_copied"], g)
                pe.wait_ge(S["prod_ready"], g * E + 4 * (r + 1))
                for j in range(4):
                    e = 4 * r + j
                    last = pe.matmul(B_Y[32 * j:32 * j + 32, :], sel[:, e, :], prod[:, e, :],
                                     start=(r == 0), stop=(r == 1))
                if r == 1:
                    last.then_inc(S["pe_y"], 1)

            def up_gate(g, n, last=False):
                bank, r = row_place(n, last)
                if n >= 2 and not last:
                    pe.wait_ge(S["c_ready"], g * GB + n - 1)
                e = pe.value_load(cexp[0:1, bass.ds(g * GB + n, 1)], min_val=0, max_val=E - 1)
                pe.matmul(bank[:, :], x1T[:, n * P:(n + 1) * P], wug[:, bass.ds(e * (2 * H2), 2 * H2)],
                          start=True, stop=False)
                pe.matmul(bank[:, :], ones[:, :], brow[:, bass.ds(e * (2 * H2) + BUG, 2 * H2)],
                          start=False, stop=True).then_inc(S["pe_ug"], 1)
                return e

            def hidden_T(g, n, last=False):
                bank, r = row_place(n, last)
                pe.wait_ge(S["hid_ready"], g * GB + n + 1)
                for c in range(2):
                    ins = pe.transpose(bank[:, c * P:(c + 1) * P], hid[:, r, c * P:(c + 1) * P], ident)
                ins.then_inc(S["pe_ht"], 1)

            def down(g, n, e, last=False):
                bank, r = row_place(n, last)
                pe.wait_ge(S["hidT_ready"], g * GB + n + 1)
                for c in range(2):
                    pe.matmul(bank[:, 0:P], hidT[:, r, c * P:(c + 1) * P],
                              wd[:, bass.ds(e * (2 * P) + c * P, P)], start=(c == 0), stop=False)
                pe.matmul(bank[:, 0:P], ones[:, :], brow[:, bass.ds(e * P + BDO, P)],
                          start=False, stop=True).then_inc(S["pe_c"], 1)

            def c_T(g):
                for n in range(GB):
                    pe.wait_ge(S["c_ready"], g * GB + n + 1)
                    last = pe.transpose(B_W[:, n * P:(n + 1) * P], c_sb[:, n * P:(n + 1) * P], ident)
                last.then_inc(S["pe_ct"], 1)

            def logits(g):
                pe.wait_ge(S["cT_ready"], g + 1)
                for n in range(GB):
                    last = pe.matmul(B_W[:, n * E:(n + 1) * E], cT[:, n * P:(n + 1) * P], wrt[:, :],
                                     start=(n == 0), stop=(n == GB - 1), skip_group_check=True)
                last.then_inc(S["pe_l"], 1)

            def x1_rows(g):
                for n in range(GB):
                    last = pe.transpose(B_Y[:, n * P:(n + 1) * P], x1T[:, n * P:(n + 1) * P], ident)
                last.then_inc(S["pe_x1"], 1)

            def ranks_of(g):
                pe.wait_ge(S["lg_copied"], g + 1)
                pe.wait_ge(S["chosen"], g + 1)
                ranks = B_W[:, 0:(GB + 1) * E].rearrange("p (b e) -> p b e", e=E)
                pe.matmul(ranks[:, 0:GB, :], bef[:, :], M[:, :, :], start=True, stop=False, skip_group_check=True)
                for i in range(GB):
                    pe.matmul(ranks[:, i + 1:, :], ones[:, :], M[:, i:i + 1, :].broadcast_to([P, GB - i, E]),
                              start=False, stop=False, skip_group_check=True)
                pe.matmul(ranks, ones[:, :], Mpre[:, :].unsqueeze(1).broadcast_to([P, GB + 1, E]),
                          start=False, stop=True, skip_group_check=True).then_inc(S["pe_rank"], 1)

            def y_T(g):
                pe.wait_ge(S["act_y"], g + 1)
                for i in range(GB):
                    last = pe.transpose(B_Y[:, i * P:(i + 1) * P], y_sb[:, i * P:(i + 1) * P], ident)
                last.then_inc(S["pe_yt"], 1)

            def z_T(g):
                pe.wait_ge(S["z_ready"], g + 1)
                for i in range(GB):
                    last = pe.transpose(B_Y[:, i * P:(i + 1) * P], z_sb[:, i * P:(i + 1) * P], ident)
                last.then_inc(S["pe_zt"], 1)

            def mix_heads(g):
                pe.wait_ge(S["act_zn"], g + 1)
                pe.matmul(B_Y[:, :], w(5), zn[:, :], start=True, stop=True).then_inc(S["pe_o"], 1)

            def step(g, first, ahead):
                gate_q(g + 1, 0)
                reduce_y(g, 1, first)
                gate_q(g + 1, 1)
                reg = {}
                if not first:
                    reg[2] = up_gate(g - 1, 2)
                y_T(g)
                if not first:
                    reg[3] = up_gate(g - 1, 3)
                if ahead:
                    project_h(g + 2)
                if not first:
                    for n in range(2, GB):
                        hidden_T(g - 1, n)
                    for n in range(2, GB):
                        down(g - 1, n, reg[n])
                z_T(g)
                if ahead:
                    project_c(g + 2)
                mix_heads(g)
                if not first:
                    c_T(g - 1)
                if ahead:
                    project_vk(g + 2, 0)
                if not first:
                    logits(g - 1)
                if first:
                    pe.wait_ge(S["s_ugd"], 16 * 2)
                    pe.wait_ge(S["s_bias_rows"], 16)
                pe.wait_ge(S["x1_ready"], g + 1)
                for n in range(2):
                    reg[n] = up_gate(g, n)
                x1_rows(g)
                if ahead:
                    project_vk(g + 2, 1)
                for n in range(2):
                    hidden_T(g, n)
                for n in range(2):
                    down(g, n, reg[n])
                reduce_y(g + 1, 0, False)
                if not first:
                    ranks_of(g - 1)
                if not ahead:
                    for n in range(2, GB):
                        up_gate(g, n)

            pe.wait_ge(S["s_wf"], 16)
            pe.wait_ge(S["s_x0"], 16)
            project_h(0)
            pe.wait_ge(S["s_wr"], 16)
            project_c(0)
            project_vk(0, 0)
            project_vk(0, 1)
            pe.wait_ge(S["s_wsp"], 16)
            for e in range(SPREAD):
                pe.matmul(spread_bank[e][:, :], wsp[:, e * P:(e + 1) * P], xc[:, :],
                          start=True, stop=True).then_inc(S["pe_spread"], 1)
                if e == 0:
                    gate_q(0, 0)
            gate_q(0, 1)
            pe.wait_ge(S["s_x"], 16)
            project_h(1)
            project_c(1)
            project_vk(1, 0)
            project_vk(1, 1)
            pe.wait_ge(S["s_small"], 16)
            pe.wait_ge(S["expert_ready"], 1)
            pe.wait_ge(S["ones_ready"], 1)
            pe.wait_ge(S["before_ready"], 1)
            def late_experts(g):
                return {n: pe.value_load(cexp[0:1, bass.ds(g * GB + n, 1)], min_val=0, max_val=E - 1) for n in (2, 3)}

            reduce_y(0, 0, True)
            step(0, True, True)
            with pe.Fori(1, NG - 2) as g:
                step(g, False, True)
            step(NG - 2, False, False)
            g = NG - 1
            late = late_experts(g - 1)
            reduce_y(g, 1, False)
            for n in range(2, GB):
                hidden_T(g - 1, n)
            y_T(g)
            for n in range(2, GB):
                down(g - 1, n, late[n])
            c_T(g - 1)
            z_T(g)
            mix_heads(g)
            logits(g - 1)
            pe.wait_ge(S["x1_ready"], g + 1)
            reg = []
            for n in range(GB):
                reg.append(up_gate(g, n, True))
                if n >= 2:
                    hidden_T(g, n - 2, True)
            down(g, 0, reg[0], True)
            ranks_of(g - 1)
            hidden_T(g, 2, True)
            down(g, 1, reg[1], True)
            hidden_T(g, 3, True)
            for n in range(2, GB):
                down(g, n, reg[n], True)
            c_T(g)
            x1_rows(g)
            logits(g)
            ranks_of(g)
            def job_in(j, r, n):
                pe.wait_ge(s_job[r], n * 16 + 16)
                if not (isinstance(j, int) and j == 0):
                    pe.wait_ge(S["jT_ready"], j)
                pe.transpose(J_X[:, 0:P], jin[:, r, 0:P], ident).then_inc(S["pe_jx"], 1)

            def expert_of(j):
                return pe.value_load(jwex[0:1, bass.ds(j, 1)], min_val=0, max_val=E - 1)

            def job_up(j, r, n, before):
                pe.wait_ge(s_w1j[r], n * 16 + 16)
                pe.wait_ge(S["jT_ready"], j + 1)
                if before is not None:
                    pe.wait_ge(S["gelu_done"], before)
                for c in range(FC):
                    last = pe.matmul(J_H[r][:, c * P:(c + 1) * P], w1j[:, r, c * P:(c + 1) * P], jT[:, r, :],
                                     start=(c == 0), stop=(c == FC - 1), skip_group_check=True)
                last.then_inc(S["pe_jh"], 1)

            def job_down(j, r, e, before):
                pe.wait_ge(S["gelu_done"], j + 1)
                if before is not None:
                    pe.wait_ge(s_put_res[r], before)
                for c in range(FC):
                    pe.matmul(J_O[r][:, 0:P], actT[:, r, c * P:(c + 1) * P],
                              w2[:, bass.ds(e * (FC * P) + c * P, P)], start=(c == 0), stop=False)
                pe.matmul(J_O[r][:, 0:P], ones[:, :], brow[:, bass.ds(e * P + B2O, P)],
                          start=False, stop=True).then_inc(S["pe_jo"], 1)

            pe.wait_ge(S["s_w2"], 16)
            pe.wait_ge(S["jobs_ready"], 1)
            job_in(0, 0, 0)
            for j in range(RING + 2):
                job_in(j + 1, (j + 1) % RING, (j + 1) // RING)
                job_up(j, j % RING, j // RING, j - 2 if j >= RING else None)
                if j >= 2:
                    job_down(j - 2, j - 2, expert_of(j - 2), None)
            for j in range(RING + 2, 2 * RING):
                job_in(j + 1, (j + 1) % RING, (j + 1) // RING)
                job_up(j, j % RING, j // RING, j - 2)
                job_down(j - 2, (j - 2) % RING, expert_of(j - 2), 1)
            with pe.Fori(1, JOBS // (2 * RING)) as u:
                for i in range(2 * RING):
                    j, r = u * (2 * RING) + i, i % RING
                    t = u * 2 + i // RING
                    job_in(j + 1, (r + 1) % RING, t + (r + 1) // RING)
                    job_up(j, r, t, j - 2)
                    job_down(j - 2, (r - 2) % RING, expert_of(j - 2), t if r == 2 else t - 1)
            for j in range(JOBS - RING, JOBS + 2):
                if j + 1 < JOBS:
                    job_in(j + 1, (j + 1) % RING, (j + 1) // RING)
                if j < JOBS:
                    job_up(j, j % RING, j // RING, j - 2)
                job_down(j - 2, (j - 2) % RING, expert_of(j - 2), (j - 2) // RING)


def kernel(x, cond_8, L0_cond_W_base, L0_cond_b_base, L0_cond_As, L0_cond_Bs, L0_attn_Wq, L0_attn_Wk, L0_attn_Wv,
           L0_attn_Wg, L0_attn_Wo, L0_attn_gamma, L0_attn_beta, L0_cond2_W_up, L0_cond2_b_up, L0_cond2_W_gate,
           L0_cond2_b_gate, L0_cond2_W_down, L0_cond2_b_down, L0_ffn_router_w, L0_ffn_w1, L0_ffn_b1, L0_ffn_w2,
           L0_ffn_b2):
    import concourse.bacc as bacc
    from concourse.bass_utils import run_bass_kernel_spmd

    a = np.asarray
    at = np.arange(P)
    yrow = (at % 16) * E + 4 * (at % 32 // 16) + at // 32
    arrays = {
        "xT": a(x).transpose(2, 0, 1).reshape(P, NT),
        "w_first": np.concatenate([a(L0_cond_W_base).T, a(L0_cond_As).reshape(P, P).T], axis=1),
        "w_rest": np.concatenate([a(L0_cond_Bs).transpose(0, 2, 1).reshape(P, P), a(L0_attn_Wv).T, a(L0_attn_Wk).T,
                                  a(L0_attn_Wg).T, a(L0_attn_Wq).T, a(L0_attn_Wo).T[yrow]], axis=1),
        "w_spread": np.concatenate([a(L0_attn_Wv).T[:, at // E * E + e] for e in range(SPREAD)], axis=1),
        "w_upgate": np.concatenate([a(L0_cond2_W_up), a(L0_cond2_W_gate)], axis=1).transpose(2, 0, 1).reshape(P, -1),
        "w_down": a(L0_cond2_W_down).reshape(E, P, 2, P).transpose(3, 0, 2, 1).reshape(P, -1),
        "w_1": a(L0_ffn_w1).transpose(0, 2, 1),
        "w_2": a(L0_ffn_w2).reshape(E, P, FC, P).transpose(3, 0, 2, 1).reshape(P, -1),
        "cond_row": a(cond_8).reshape(1, -1),
        "cond_T": a(cond_8).T,
    }
    select = np.zeros((P, E, 32), np.float32)
    for e in range(E):
        select[at, e, 16 * (e // 4) + at // E] = 1
    ranks = np.tile(np.concatenate([E - np.arange(E), REGION * np.arange(E)]).astype(np.float32), (P, 1))
    columns = np.stack([a(L0_cond_b_base), a(L0_attn_gamma)[yrow], a(L0_attn_beta)[yrow]], axis=1)
    biases = np.concatenate([np.concatenate([a(L0_cond2_b_up), a(L0_cond2_b_gate)], axis=1).reshape(-1),
                             a(L0_cond2_b_down).reshape(-1),
                             a(L0_ffn_b2).reshape(-1)]).reshape(P, -1)
    arrays["small"] = np.concatenate([np.eye(P, dtype=np.float32), select.reshape(P, -1),
                                      np.triu(np.ones((P, P), np.float32), 1), ranks, a(L0_ffn_router_w).T,
                                      columns, a(L0_ffn_b1).reshape(E * FC, P).T, biases], axis=1)
    row = np.arange(NB)
    arrays["dest"] = (GB * at[:, None, None] + (row // GB * GT + row % GB)[None, :, None]
                      + NT * np.arange(TOPK)[None, None, :]).astype(np.uint32).reshape(P, -1)
    arrays["job_no"] = np.stack([np.arange(JOBS), P * np.arange(JOBS)]).astype(np.float32).reshape(1, -1)

    nc = bacc.Bacc("TRN2", target_bir_lowering=False, num_devices=1)
    arrays = {k: np.ascontiguousarray(v) for k, v in arrays.items()}
    aps = {k: nc.dram_tensor(k, list(v.shape), mybir.dt.from_np(v.dtype), kind="ExternalInput").ap()
           for k, v in arrays.items()}
    out = nc.dram_tensor("out", [NB, P, P], F32, kind="ExternalOutput").ap()
    adaln_attn_ffn_kernel(nc, out=out, **aps)
    r = run_bass_kernel_spmd(nc, [arrays], core_ids=[0])
    return r.results[0]["out"]
```
